# Optimizing a Trainium2 kernel written in Bass

```python
import numpy as np
import jax
import jax.numpy as jnp

def _softmax(x, axis=-1):
    return jax.nn.softmax(x, axis=axis)

def _gelu(x):
    return jax.nn.gelu(x, approximate=True)

def _silu(x):
    return jax.nn.silu(x)

def _sigmoid(x):
    return jax.nn.sigmoid(x)

def _layernorm(x, axis=-1, eps=1e-05):
    m = jnp.mean(x, axis=axis, keepdims=True)
    v = jnp.var(x, axis=axis, keepdims=True)
    return (x - m) / jnp.sqrt(v + eps)

def _scatter_add(tgt, idx, src, axis=0):
    return tgt.at[idx].add(src)

def _segment_sum(src, seg, n):
    return jax.ops.segment_sum(src, seg, n)
kernel_name = 'mk_prb_d1_jaxref_r4_78d7f6'

def setup_inputs(seed: int=0):
    np.random.seed(seed)
    _w = jnp.asarray

    def _L0_attn_setup():
        import jax, jax.numpy as jnp
        import numpy as np
        D_MODEL = 256
        D_STATE = 16
        D_CONV = 4
        EXPAND = 2
        D_INNER = D_MODEL * EXPAND
        B_SZ = 2
        SEQ = 1024
        key = jax.random.key(seed)
        ks = jax.random.split(key, 11)
        rn = lambda i, shape, scale=1.0: jax.random.normal(ks[i], shape, jnp.float32) * scale
        return {'x': rn(0, (B_SZ, SEQ, D_MODEL)), 'W_in': rn(1, (D_MODEL, D_INNER), D_MODEL ** (-0.5)), 'b_in': rn(2, (D_INNER,), 0.01), 'conv_w': rn(3, (D_INNER, 1, D_CONV), 0.1), 'conv_b': rn(4, (D_INNER,), 0.01), 'A': rn(5, (D_STATE, D_STATE), 0.1), 'Bp': rn(6, (D_STATE,)), 'Cp': rn(7, (D_STATE,)), 'Dp': rn(8, (1,)), 'W_out': rn(9, (D_INNER, D_MODEL), D_INNER ** (-0.5)), 'b_out': rn(10, (D_MODEL,), 0.01)}
    _L0_attn_in = _L0_attn_setup()

    def _L0_ffn_setup():
        import jax, jax.numpy as jnp
        import numpy as np
        NUM_HEADS = 16
        TOP_K = 2
        key = jax.random.key(seed)
        ks = jax.random.split(key, 5)
        B, S, D, E = (4, 512, 256, 8)
        scale = 0.02
        return {'x': jax.random.normal(ks[0], (B, S, D), dtype=jnp.float32), 'W_qkv': jax.random.normal(ks[1], (D, 3 * D), dtype=jnp.float32) * scale, 'b_qkv': jnp.zeros((3 * D,), dtype=jnp.float32), 'W_gate': jax.random.normal(ks[2], (D, E), dtype=jnp.float32) * scale, 'b_gate': jnp.zeros((E,), dtype=jnp.float32), 'W_experts': jax.random.normal(ks[3], (E, D, D), dtype=jnp.float32) * scale, 'b_experts': jnp.zeros((E, D), dtype=jnp.float32)}
    _L0_ffn_in = _L0_ffn_setup()
    _d = {'L0_attn_x': _L0_attn_in['x'], 'L0_attn_W_in': _L0_attn_in['W_in'], 'L0_attn_b_in': _L0_attn_in['b_in'], 'L0_attn_conv_w': _L0_attn_in['conv_w'], 'L0_attn_conv_b': _L0_attn_in['conv_b'], 'L0_attn_A': _L0_attn_in['A'], 'L0_attn_Bp': _L0_attn_in['Bp'], 'L0_attn_Cp': _L0_attn_in['Cp'], 'L0_attn_Dp': _L0_attn_in['Dp'], 'L0_attn_W_out': _L0_attn_in['W_out'], 'L0_attn_b_out': _L0_attn_in['b_out'], 'L0_ffn_W_qkv': _L0_ffn_in['W_qkv'], 'L0_ffn_b_qkv': _L0_ffn_in['b_qkv'], 'L0_ffn_W_gate': _L0_ffn_in['W_gate'], 'L0_ffn_b_gate': _L0_ffn_in['b_gate'], 'L0_ffn_W_experts': _L0_ffn_in['W_experts'], 'L0_ffn_b_experts': _L0_ffn_in['b_experts']}
    _x0 = _d['L0_attn_x']
    _d['L0_attn_x'] = jax.random.normal(jax.random.fold_in(jax.random.key(seed), 1), (8, 512, 256), dtype=_x0.dtype)
    del _x0
    return _d

def reference(L0_attn_x, L0_attn_W_in, L0_attn_b_in, L0_attn_conv_w, L0_attn_conv_b, L0_attn_A, L0_attn_Bp, L0_attn_Cp, L0_attn_Dp, L0_attn_W_out, L0_attn_b_out, L0_ffn_W_qkv, L0_ffn_b_qkv, L0_ffn_W_gate, L0_ffn_b_gate, L0_ffn_W_experts, L0_ffn_b_experts):

    def _L0_attn_ref(x, W_in, b_in, conv_w, conv_b, A, Bp, Cp, Dp, W_out, b_out):
        import jax, jax.numpy as jnp
        import numpy as np
        D_MODEL = 256
        D_STATE = 16
        D_CONV = 4
        EXPAND = 2
        D_INNER = D_MODEL * EXPAND
        B_SZ = 2
        SEQ = 1024
        Bsz, S, _ = x.shape
        d_inner = W_in.shape[1]
        u = x @ W_in + b_in
        u = u.transpose(0, 2, 1)
        u = jax.lax.conv_general_dilated(u, conv_w, window_strides=(1,), padding=[(D_CONV - 1, 0)], dimension_numbers=('NCH', 'OIH', 'NCH'), feature_group_count=d_inner) + conv_b[None, :, None]
        u = u.transpose(0, 2, 1)
        At = jnp.tanh(A)

        def step(h, u_t):
            h = jnp.einsum('ij,bdj->bdi', At, h) + u_t[..., None] * Bp
            y = jnp.einsum('j,bdj->bd', Cp, h) + Dp[0] * u_t
            return (h, y)
        h0 = jnp.zeros((Bsz, d_inner, Bp.shape[0]), x.dtype)
        _, ys = jax.lax.scan(step, h0, u.transpose(1, 0, 2))
        y = jax.nn.silu(ys.transpose(1, 0, 2))
        return y @ W_out + b_out

    def _L0_ffn_ref(x, W_qkv, b_qkv, W_gate, b_gate, W_experts, b_experts):
        import jax, jax.numpy as jnp
        import numpy as np
        NUM_HEADS = 16
        TOP_K = 2
        B, S, D = x.shape
        H = NUM_HEADS
        hd = D // H
        E = W_gate.shape[-1]
        qkv = (x @ W_qkv + b_qkv).reshape(B, S, 3, H, hd)
        q, k, v = (qkv[:, :, 0], qkv[:, :, 1], qkv[:, :, 2])
        attn = jnp.einsum('bqhd,bkhd->bhqk', q, k) / jnp.sqrt(jnp.asarray(hd, x.dtype))
        attn = jax.nn.softmax(attn, axis=-1)
        attn_out = jnp.einsum('bhqk,bkhd->bqhd', attn, v).reshape(B, S, D)
        gate = jax.nn.softmax(x @ W_gate + b_gate, axis=-1)
        top_g, top_i = jax.lax.top_k(gate, TOP_K)
        combine = jnp.sum(jax.nn.one_hot(top_i, E, dtype=x.dtype) * top_g[..., None], axis=2)
        expert_out = jnp.einsum('bsd,edf->bsef', x, W_experts) + b_experts
        moe_out = jnp.einsum('bsef,bse->bsf', expert_out, combine)
        return attn_out + moe_out
    x = L0_attn_x
    xn = _layernorm(x, axis=-1)
    x = x + _L0_attn_ref(xn, L0_attn_W_in, L0_attn_b_in, L0_attn_conv_w, L0_attn_conv_b, L0_attn_A, L0_attn_Bp, L0_attn_Cp, L0_attn_Dp, L0_attn_W_out, L0_attn_b_out) + _L0_ffn_ref(xn, L0_ffn_W_qkv, L0_ffn_b_qkv, L0_ffn_W_gate, L0_ffn_b_gate, L0_ffn_W_experts, L0_ffn_b_experts)
    return x

_drawn_inputs = setup_inputs


def setup_inputs(seed=0):
    import zlib

    import numpy as np

    out = dict(_drawn_inputs(seed))
    spreads = {'L0_ffn_b_qkv': (0.0, 0.1),
     'L0_ffn_b_gate': (0.0, 0.273),
     'L0_ffn_b_experts': (0.0, 0.361)}
    factors = {'L0_attn_b_in': 8.0, 'L0_attn_b_out': 6.082, 'L0_ffn_W_qkv': 4.433}
    for name, (base, spread) in spreads.items():
        noise = np.random.default_rng([zlib.crc32(name.encode()), seed]).standard_normal(out[name].shape)
        drawn = base * np.exp(spread * noise) if base else spread * noise
        out[name] = jnp.asarray(drawn.astype(out[name].dtype))
    for name, factor in factors.items():
        out[name] = (out[name] * factor).astype(out[name].dtype)
    return out
```

```python
from contextlib import ExitStack

import concourse.bass as bass
from concourse import mybir

F32 = mybir.dt.float32
F32R = mybir.dt.float32r
ALU = mybir.AluOpType
ACT = mybir.ActivationFunctionType
AX = mybir.AxisListType

NB = 8
S = 512
D = 256
NG = 4 * NB
NI = 16 * NG
ST_LAG = 21
PV_LAG = ST_LAG + 3
NP = 6
NE = 8


class Marks:

    def __init__(self):
        self.at = {}

    def name(self, key, sem, value):
        assert key not in self.at, key
        self.at[key] = (sem, value)


class Queue:

    def __init__(self, marks, sem):
        self.marks, self.sem, self.count, self.ops = marks, sem, 0, []

    def do(self, fn, needs=(), tell=None):
        if tell is not None:
            self.count += 1
            self.marks.name(tell, self.sem, self.count)
        self.ops.append((fn, list(needs), self.sem if tell is not None else None, 1))

    def dma(self, fn, needs, tell, sem, counts):
        counts[sem.name] = counts.get(sem.name, 0) + 16
        self.marks.name(tell, sem, counts[sem.name])
        self.ops.append((fn, list(needs), sem, 16))

    def emit(self, eng):
        seen = {}
        for fn, needs, sem, inc in self.ops:
            most = {}
            for key in needs:
                s, v = self.marks.at[key]
                if v > most.get(s.name, (s, 0))[1]:
                    most[s.name] = (s, v)
            for s, v in most.values():
                if seen.get(s.name, 0) < v:
                    eng.wait_ge(s, v)
                    seen[s.name] = v
            ins = fn(eng)
            if sem is not None:
                ins.then_inc(sem, inc)


def program(nc, x, wqk, bqk, wvg, bv, bg, win, bin_, cw, cb, A, AT, Bp, Cp, Dp, wout, bout, wexp, bexp, out, kd, rd):
    ctx = ExitStack()
    with ctx:
        def sb(name, shape, dt=F32):
            return ctx.enter_context(nc.sbuf_tensor(name, shape, dt))

        def sem(name):
            return ctx.enter_context(nc.semaphore(name))

        PS = [ctx.enter_context(nc.psum_tensor(f"PS{i}", [128, 512], F32)) for i in range(8)]
        SB, TB, OB, FB = PS[0:2], PS[2:4], PS[4:6], PS[6:8]

        qst = sb("qst", [98, 3, 4, 512], F32R)
        kst = sb("kst", [98, 3, 4, 512], F32R)
        Pt = sb("Pt", [128, NP, 512])
        qkh = sb("qkh", [128, 2, 512], F32R)
        qkl = sb("qkl", [128, 2, 512], F32R)
        wqkh = sb("wqkh", [128, 2, 512], F32R)
        wqkl = sb("wqkl", [128, 2, 512], F32R)
        wvh = sb("wvh", [128, 2, 264], F32R)
        wvl = sb("wvl", [128, 2, 264], F32R)
        winh = sb("winh", [128, 2, 512], F32R)
        winl = sb("winl", [128, 2, 512], F32R)
        wouth = sb("wouth", [128, 4, 256], F32R)
        woutl = sb("woutl", [128, 4, 256], F32R)
        weh = sb("weh", [128, 2, 2048], F32R)
        wel = sb("wel", [128, 2, 2048], F32R)
        Rh = sb("Rh", [128, 640], F32R)
        Rl = sb("Rl", [128, 640], F32R)
        Bt = sb("Bt", [128, 4, 512])
        V = sb("V", [128, 2, 4, 16, 17])
        acc = sb("acc", [128, 3, 4, 256])
        xTh = sb("xTh", [128, 2, 512], F32R)
        xTl = sb("xTl", [128, 2, 512], F32R)
        xn = sb("xn", [128, 4, 256])
        xh = sb("xh", [128, 1024], F32R)
        xl = sb("xl", [128, 1024], F32R)
        yh = sb("yh", [128, 2, 512], F32R)
        yl = sb("yl", [128, 2, 512], F32R)
        ys = sb("ys", [128, 2, 512])
        th = sb("th", [128, 512])
        ot = sb("ot", [128, 512])
        ident = sb("ident", [128, 128])
        bvb = sb("bvb", [128, 256])
        boutb = sb("boutb", [128, 256])
        bgb = sb("bgb", [128, 8])
        be = sb("be", [8, 256])
        cpad = sb("cpad", [128, 4, 8])
        cT = sb("cT", [8, 512])
        wr = sb("wr", [128, 8])
        mx = sb("mx", [128, 2, 16])
        mh = sb("mh", [16, 128], F32R)
        ml = sb("ml", [16, 128], F32R)
        st6 = sb("st6", [128, 4, 6])
        mv = sb("mv", [128, 4, 2])
        rs = sb("rs", [128, 4])
        ve = sb("ve", [128, 4])
        mhalf = sb("mhalf", [128, 4])
        rc = sb("rc", [128, 16])
        at = sb("at", [128, 256])
        bq = sb("bq", [128, 4])
        binc = sb("binc", [128, 4])
        cwc = sb("cwc", [128, 4, 4])
        cbc = sb("cbc", [128, 4])
        bw = sb("bw", [128, 4, 4])
        G = sb("G", [128, 10, 4, 8])
        g4 = sb("g4", [128, 6, 4])
        am = sb("am", [16, 2, 16])
        Pm = sb("Pm", [16, 2, 32])
        cpc = sb("cpc", [16, 1])
        V0 = th[0:16, :]
        kp = ys[0:1, :, :].rearrange("p a c -> p (a c)")[:, 0:768]
        dpc = sb("dpc", [1, 1])

        xhn = xh[:, :].rearrange("p (a c) -> p a c", a=4)
        xln = xl[:, :].rearrange("p (a c) -> p a c", a=4)
        zh = xh[:, :].rearrange("p (a c) -> p a c", a=2)
        zl = xl[:, :].rearrange("p (a c) -> p a c", a=2)
        Rraw = ys[:, :, :].rearrange("p a c -> p (a c)")[:, 0:640]
        onesf = ot[:, 0:128]

        marks = Marks()
        counts = {}
        PE, DV, AC, PO, SP = (Queue(marks, sem(f"s_{n}")) for n in ("pe", "dve", "act", "pool", "sp"))
        s_w = [sem(f"s_w{i}") for i in range(8)]
        s_c = [sem(f"s_c{i}") for i in range(13)]
        s_x = [sem(f"s_x{i}") for i in range(3)]
        s_st = [sem(f"s_st{i}") for i in range(3)]
        s_m = [sem(f"s_m{i}") for i in range(3)]
        s_k = sem("s_k")
        s_o = sem("s_o")

        def F(ap):
            return ap.bitcast(F32)

        def dma(q, dst, src, needs, tell, s):
            q.dma(lambda e: e.dma_start(dst, src), needs, tell, s, counts)

        def load_x(b, q=SP):
            dma(q, acc[:, b % 3, :, :], x[b].rearrange("(a p) d -> p a d", p=128),
                [("store", b - 3)] if b >= 3 else [[], [("wl", "we2")], [("wl", "out")]][b], ("x", b), s_x[b % 3])

        def kp_rows(w):
            return w.rearrange("(k p) n -> p k n", p=128)

        stages = [
            ("qk", Pt[:, 0:2, :], wqk, wqkh, wqkl, 1.0),
            ("vg", Pt[:, 2:4, :].rearrange("p a c -> p (a c)")[:, 0:528].rearrange("p (k n) -> p k n", k=2),
             wvg, wvh, wvl, 1.0),
            ("we0", Bt[:, 0:2, :], wexp[:, 0:512], weh[:, :, 0:512], wel[:, :, 0:512], 1.0),
            ("we1", Bt[:, 2:4, :], wexp[:, 512:1024], weh[:, :, 512:1024], wel[:, :, 512:1024], 1.0),
            ("in", Pt[:, 4:6, :], win, winh, winl, 1.0),
            ("out", acc[:, 2, :, :], wout, wouth, woutl, 0.5),
            ("we2", acc[:, 1, :, :].rearrange("p a c -> p (a c)").rearrange("p (k n) -> p k n", k=2),
             wexp[:, 1024:1536], weh[:, :, 1024:1536], wel[:, :, 1024:1536], 1.0),
            ("we3", xn[:, :, :].rearrange("p a c -> p (a c)").rearrange("p (k n) -> p k n", k=2),
             wexp[:, 1536:2048], weh[:, :, 1536:2048], wel[:, :, 1536:2048], 1.0),
        ]
        load_x(0)
        small = [
            (am[:, 0, :], A), (am[:, 1, :], AT), (V0[:, 0:1], Bp.rearrange("(p o) -> p o", o=1)),
            (cpc[:, :], Cp.rearrange("(p o) -> p o", o=1)), (dpc[:, :], Dp.rearrange("(p o) -> p o", o=1)),
            (bq[:, :], bqk), (bvb[:, :], bv), (bgb[:, :], bg),
            (binc[:, :], bin_), (cwc[:, :, :], cw), (cbc[:, :], cb), (boutb[:, :], bout),
        ]
        names = ["A", "AT", "Bp", "Cp", "Dp", "bq", "bv", "bg", "bin", "cw", "cb", "bout"]
        for n, (dst, src) in enumerate(small[:5]):
            dma(PO, dst, src, [], ("c", names[n]), s_c[n])
        for n, (key, stg, src, hi, lo, sc) in enumerate(stages[:7]):
            dma(SP if n % 2 == 0 else AC, stg, kp_rows(src), [], ("w", key), s_w[n])
            if n == 1:
                for i in (5, 6, 7):
                    dma(SP, small[i][0], small[i][1], [], ("c", names[i]), s_c[i])
        for i in range(8, 12):
            dma(SP, small[i][0], small[i][1], [], ("c", names[i]), s_c[i])
        dma(SP, be[:, :], bexp, [], ("c", "be"), s_c[12])

        PO.do(lambda e: e.memset(mhalf[:, :], -0.5), [], ("mhalf",))
        PO.do(lambda e: e.memset(ident[:, :], 0.0), [], ("id0",))
        PO.do(lambda e: e.affine_select(out=ident[:, :], in_=ident[:, :], compare_op=ALU.not_equal, fill=1.0,
                                        base=0, pattern=[[-1, 128]], channel_multiplier=1),
              [("id0",)], ("ident",))
        for k in range(8):
            PO.do(lambda e, k=k: e.memset(wr[:, k:k + 1], float(8 - k)), [], ("wr",) if k == 7 else None)
        PO.do(lambda e: e.memset(kp, 0.0), [], ("kp0",))
        PO.do(lambda e: e.memset(onesf, 1.0), [], ("ones",))
        PO.do(lambda e: e.memset(F(qst[64:96, :, :, :]), 0.0), [("ones",)], ("qpad",))
        PO.do(lambda e: e.memset(F(kst[64:96, :, :, :]), 0.0), [("qpad",)], ("kpad",))
        PO.do(lambda e: e.memset(F(kst[96:98, :, :, :]), -1.0), [("kpad",)], ("kneg",))
        PO.do(lambda e: e.memset(V[:, :, :, :, 16:17], 1.0), [("kneg",)], ("vone",))
        for i in range(2):
            DV.do(lambda e, i=i: e.memset(OB[i][:, :], 0.0), [], ("oz", i))

        def split(n, eng):
            key, stg, src, hi, lo, sc = stages[n]
            AC.do(lambda e: e.activation(hi[:, :, :] if key[0:2] != "we" else hi, stg, ACT.Copy, scale=sc),
                  [("w", key)], ("wh", key))
            h = hi[:, :, :] if key[0:2] != "we" else hi
            lw = lo[:, :, :] if key[0:2] != "we" else lo
            if sc != 1.0:
                for a in range(4):
                    eng.do(lambda e, a=a: e.scalar_tensor_tensor(out=lw[:, a, :], in0=stg[:, a, :], scalar=sc,
                                                                 in1=F(h)[:, a, :], op0=ALU.mult,
                                                                 op1=ALU.subtract),
                           [("wh", key)], ("wl", key) if a == 3 else None)
            else:
                eng.do(lambda e: e.tensor_tensor(lw, stg, F(h), ALU.subtract), [("wh", key)], ("wl", key))

        def ln_stats(b, a):
            xa = acc[:, b % 3, a, :]
            DV.do(lambda e: e.bn_stats(st6[:, a, :], xa), [("x", b)], ("bn", b, a))
            DV.do(lambda e: e.bn_aggr(mv[:, a, :], st6[:, a, :]),
                  [("bn", b, a)] + ([("xn", b - 1, a)] if b else []), ("ag", b, a))
            if a == 3:
                DV.do(lambda e: e.tensor_scalar(ve[:, :], mv[:, :, 1], 1e-5, None, ALU.add),
                      [("ag", b, i) for i in range(4)], ("ve", b))
                PO.do(lambda e: e.tensor_tensor(rs[:, :], ve[:, :], mhalf[:, :], ALU.pow),
                      [("ve", b), ("mhalf",)], ("rs", b))

        def ln_norm(b, a):
            xa = acc[:, b % 3, a, :]
            DV.do(lambda e: e.tensor_scalar(xn[:, a, :], xa, mv[:, a, 0:1], rs[:, a:a + 1],
                                            ALU.subtract, ALU.mult),
                  [("rs", b)] + ([("xl", b - 1, a), ("T", b - 1, 1)] if b else []), ("xn", b, a))
            free = [("Y", b - 1, 3)] if b else []
            PO.do(lambda e: e.tensor_copy(xhn[:, a, :], xn[:, a, :]), [("xn", b, a)] + free, ("xh", b, a))
            PO.do(lambda e: e.tensor_tensor(xln[:, a, :], xn[:, a, :], F(xhn[:, a, :]), ALU.subtract),
                  [("xh", b, a)], ("xl", b, a))
            PO.do(lambda e: e.tensor_tensor(xa, xa, boutb[:, :], ALU.add), [("xn", b, a), ("c", "bout")],
                  ("ax", b, a))

        fill = {"n": 0, "read": [[], []]}

        def bank():
            i = fill["n"] % 2
            fill["n"] += 1
            needs, fill["read"][i] = fill["read"][i], []
            return i, FB[i], needs

        def three(P, pairs, tell, needs, start=True, stop=True):
            n = 3 * len(pairs)
            k = 0
            for (lh, ll), (rh, rl) in pairs:
                for u, v in ((lh, rh), (ll, rh), (lh, rl)):
                    PE.do(lambda e, u=u, v=v, k=k: e.matmul(P, u, v, start=(start and k == 0),
                                                            stop=(stop and k == n - 1)),
                          needs if k == 0 else [], tell if k == n - 1 else None)
                    k += 1

        def unit_T(b, f):
            i, P, needs = bank()
            for a in range(4):
                PE.do(lambda e, a=a: e.transpose(P[:, 128 * a:128 * a + 128], xn[:, a, 128 * f:128 * f + 128],
                                                 ident[:, :]),
                      needs + [("xn", b, a), ("ident",)], ("T", b, f) if a == 3 else None)
            free = [("M", b - 1, 15), ("QK", b - 1, 1, 1)] if b else []
            AC.do(lambda e: e.copy(xTh[:, f, :], P[:, :]), [("T", b, f)] + free, ("xTh", b, f))
            DV.do(lambda e: e.tensor_tensor(xTl[:, f, :], P[:, :], F(xTh[:, f, :]), ALU.subtract),
                  [("xTh", b, f)], ("xTl", b, f))
            fill["read"][i] = [("xTl", b, f)]

        def xT_ready(b):
            return [("xTh", b, 0), ("xTh", b, 1), ("xTl", b, 0), ("xTl", b, 1)]

        def unit_V(b, a):
            i, P, needs = bank()
            ts = slice(128 * a, 128 * a + 128)
            three(P[:, 0:264], [((xTh[:, f, ts], xTl[:, f, ts]), (wvh[:, f, :], wvl[:, f, :])) for f in range(2)],
                  ("V", b, a), needs + xT_ready(b) + [("wh", "vg"), ("wl", "vg")])
            DV.do(lambda e: e.tensor_tensor(V[:, b % 2, a, :, 0:16],
                                            P[:, 0:256].rearrange("p (h d) -> p h d", h=16),
                                            bvb[:, :].rearrange("p (h d) -> p h d", h=16), ALU.add),
                  [("V", b, a), ("c", "bv")] + ([("PV", 64 * (b - 2) + 63)] if b >= 2 else []), ("Vs", b, a))
            DV.do(lambda e: e.tensor_tensor(G[:, 0, a, :], P[:, 256:264], bgb[:, :], ALU.add),
                  [("V", b, a), ("c", "bg")] + ([("g", b - 1, "c")] if b else []), ("lg", b, a))
            fill["read"][i] = [("Vs", b, a), ("lg", b, a)]
            if a == 3:
                gate(b)

        def gate(b):
            def bc(v):
                return v.unsqueeze(2).to_broadcast([128, 4, 8])

            def step(key, fn, needs):
                DV.do(fn, [("g", b, k) for k in needs], ("g", b, key))

            DV.do(lambda e: e.tensor_reduce(g4[:, 0, :], G[:, 0, :, :], AX.X, ALU.max),
                  [("lg", b, a) for a in range(4)], ("g", b, "m"))
            step("s", lambda e: e.tensor_tensor(G[:, 1, :, :], G[:, 0, :, :], bc(g4[:, 0, :]), ALU.subtract), ["m"])
            AC.do(lambda e: e.activation(G[:, 2, :, :], G[:, 1, :, :], ACT.Exp), [("g", b, "s")], ("g", b, "e"))
            step("z", lambda e: e.tensor_reduce(g4[:, 1, :], G[:, 2, :, :], AX.X, ALU.add), ["e"])
            step("r", lambda e: e.reciprocal(g4[:, 2, :], g4[:, 1, :]), ["z"])
            step("g", lambda e: e.tensor_tensor(G[:, 3, :, :], G[:, 2, :, :], bc(g4[:, 2, :]), ALU.mult), ["r"])
            src, val = 3, "g"
            wrb = wr[:, :].unsqueeze(1).to_broadcast([128, 4, 8])
            for r in range(2):
                step(f"x{r}", lambda e, src=src: e.tensor_reduce(g4[:, 3, :], G[:, src, :, :], AX.X, ALU.max),
                     [val] if r == 0 else [val, "q0"])
                step(f"q{r}", lambda e, src=src: e.tensor_tensor(G[:, 4, :, :], G[:, src, :, :],
                                                                 bc(g4[:, 3, :]), ALU.is_ge),
                     [f"x{r}"] + (["k0"] if r else []))
                DV.do(lambda e: e.tensor_tensor(G[:, 5, :, :], G[:, 4, :, :], wrb, ALU.mult),
                      [("g", b, f"q{r}"), ("wr",)], ("g", b, f"w{r}"))
                step(f"y{r}", lambda e: e.tensor_reduce(g4[:, 4, :], G[:, 5, :, :], AX.X, ALU.max), [f"w{r}"])
                step(f"k{r}", lambda e, r=r: e.tensor_tensor(G[:, 6 + r, :, :], G[:, 5, :, :], bc(g4[:, 4, :]),
                                                             ALU.is_equal), [f"y{r}"])
                if r == 0:
                    step("d", lambda e: e.scalar_tensor_tensor(out=G[:, 8, :, :], in0=G[:, 6, :, :], scalar=-2.0,
                                                               in1=G[:, 3, :, :], op0=ALU.mult, op1=ALU.add),
                         ["k0"])
                    src, val = 8, "d"
            step("t", lambda e: e.tensor_tensor(G[:, 9, :, :], G[:, 6, :, :], G[:, 7, :, :], ALU.add), ["k1"])
            free = [("M", b - 1, 15), ("g", b - 1, "u"), ("Ms", b - 1, 15)] if b else []
            DV.do(lambda e: e.tensor_tensor(cpad[:, :, :], G[:, 3, :, :], G[:, 9, :, :], ALU.mult),
                  [("g", b, "t")] + free, ("g", b, "c"))

        def unit_C(b):
            i, P, needs = bank()
            for a in range(4):
                PE.do(lambda e, a=a: e.transpose(P[0:8, 128 * a:128 * a + 128], cpad[:, a, :], ident[:, :]),
                      needs + [("g", b, "c"), ("ident",)] if a == 0 else [], ("g", b, "u") if a == 3 else None)
            DV.do(lambda e: e.tensor_copy(cT[:, :], P[0:8, :]),
                  [("g", b, "u")] + ([("O", b - 1, 0, 1)] if b else []), ("cT", b))
            fill["read"][i] = [("cT", b)]

        def unit_QK(b, half, w):
            i, P, needs = bank()
            m = 2 * w + half
            cs = slice(128 * m, 128 * m + 128)
            three(P[:, :], [((wqkh[:, f, cs], wqkl[:, f, cs]), (xTh[:, f, :], xTl[:, f, :])) for f in range(2)],
                  ("QK", b, half, w), needs + xT_ready(b) + [("wh", "qk"), ("wl", "qk")])
            g = 4 * b + 2 * half
            free = [("st", g - 1, k) for k in range(8)] if g else []
            AC.do(lambda e: e.activation(qkh[:, w, :], P[:, :], ACT.Identity, bias=bq[:, m:m + 1]),
                  [("QK", b, half, w), ("c", "bq")] + free, ("qkh", b, half, w))
            DV.do(lambda e: e.scalar_tensor_tensor(out=qkl[:, w, :], in0=P[:, :], scalar=bq[:, m:m + 1],
                                                   in1=F(qkh[:, w, :]), op0=ALU.add, op1=ALU.subtract),
                  [("qkh", b, half, w), ("c", "bq")] + free, ("qkl", b, half, w))
            fill["read"][i] = [("qkl", b, half, w)]

        def unit_Z(b, f):
            i, P, needs = bank()
            fs = slice(128 * f, 128 * f + 128)
            k = 0
            for c, (lo, n, r) in enumerate(((0, 512, 128), (128, 384, 128), (256, 256, 128), (256, 256, 0))):
                for u, v in ((xhn, Rh), (xln, Rh), (xhn, Rl)):
                    PE.do(lambda e, c=c, lo=lo, n=n, r=r, u=u, v=v, k=k: e.matmul(
                        P[:, lo:lo + n], u[:, c, fs], v[:, r:r + n], start=(k == 0), stop=(k == 11)),
                        needs + [("xh", b, 3), ("xl", b, 3), ("Rh",), ("Rl",)] if k == 0 else [],
                        ("Z", b, f) if k == 11 else None)
                    k += 1
            fill["read"][i] = [("zl", b, f)]
            if f == 1:
                for g in range(2):
                    j = (i + 1 + g) % 2
                    Q = FB[j]
                    AC.do(lambda e, g=g, Q=Q: e.copy(zh[:, g, :], Q[:, :]), [("Z", b, 0), ("Z", b, 1)],
                          ("zh", b, g))
                    DV.do(lambda e, g=g, Q=Q: e.tensor_tensor(zl[:, g, :], Q[:, :], F(zh[:, g, :]), ALU.subtract),
                          [("zh", b, g)], ("zl", b, g))

        def unit_Y(b, d):
            i, P, needs = bank()
            ds = slice(128 * d, 128 * d + 128)
            three(P[:, :], [((winh[:, f, ds], winl[:, f, ds]), (zh[:, f, :], zl[:, f, :])) for f in range(2)],
                  ("Y", b, d), needs + [("zh", b, 0), ("zh", b, 1), ("zl", b, 0), ("zl", b, 1),
                                        ("wh", "in"), ("wl", "in")])
            y = ys[:, d % 2, :]
            prev = ("y", b, d - 2) if d >= 2 else (("y", b - 1, d + 2) if b else ("s_ready",))
            DV.do(lambda e: e.scalar_tensor_tensor(out=y, in0=P[:, :], scalar=cwc[:, d, 3:4], in1=Bt[:, d, :],
                                                   op0=ALU.mult, op1=ALU.add),
                  [("Y", b, d), ("B", d), prev, ("c", "cw")], ("v", b, d, 0))
            for s in (1, 2, 3):
                DV.do(lambda e, s=s: e.scalar_tensor_tensor(out=y[:, s:512], in0=P[:, 0:512 - s],
                                                            scalar=cwc[:, d, 3 - s:4 - s], in1=y[:, s:512],
                                                            op0=ALU.mult, op1=ALU.add),
                      [("v", b, d, s - 1)], ("v", b, d, s))
            fill["read"][i] = [("v", b, d, 3)]
            n = 4 * b + d
            last = ("yl", n - 1) if n else None
            AC.do(lambda e: e.activation(th[:, :], y, ACT.Tanh, scale=0.5),
                  [("v", b, d, 3)] + ([last, ("yh", n - 1)] if last else [("B", k) for k in range(4)]), ("th", b, d))
            DV.do(lambda e: e.scalar_tensor_tensor(out=th[:, :], in0=th[:, :], scalar=1.0, in1=y,
                                                   op0=ALU.add, op1=ALU.mult), [("th", b, d)], ("y", b, d))
            hb, half = d % 2, d // 2
            free = []
            if half == 1:
                free = [("O", b, 0, 0), ("O", b, 0, 1)]
            elif b:
                free = [("O", b - 1, 1, 0), ("O", b - 1, 1, 1)]
            AC.do(lambda e: e.copy(yh[:, hb, :], th[:, :]), [("y", b, d)] + free, ("yh", n))
            PO.do(lambda e: e.tensor_tensor(yl[:, hb, :], th[:, :], F(yh[:, hb, :]), ALU.subtract),
                  [("yh", n)] + free, ("yl", n))

        def bias_tile(d):
            sr = SR
            DV.do(lambda e: e.tensor_scalar(bw[:, d, :], cwc[:, d, :], binc[:, d:d + 1], None, ALU.mult),
                  [("c", "cw"), ("c", "bin")], ("bw", d))
            DV.do(lambda e: e.tensor_scalar(Bt[:, d, :], sr, cbc[:, d:d + 1], None, ALU.mult),
                  [("sr",), ("c", "cb"), ("wl", "we0"), ("wl", "we1")], ("B", d, -1))
            for s in range(4):
                DV.do(lambda e, s=s: e.scalar_tensor_tensor(out=Bt[:, d, s:512], in0=sr[:, 0:512 - s],
                                                            scalar=bw[:, d, 3 - s:4 - s], in1=Bt[:, d, s:512],
                                                            op0=ALU.mult, op1=ALU.add),
                      [("bw", d), ("B", d, s - 1)], ("B", d, s) if s < 3 else ("B", d))

        def unit_O(b, half, a2):
            i, P, needs = bank()
            ready = [("yh", 4 * b + 2 * half + k) for k in range(2)] + [("yl", 4 * b + 2 * half + k) for k in range(2)]
            ready += [("wh", "out"), ("wl", "out")]
            for a in (2 * a2, 2 * a2 + 1):
                o = P[:, 256 * (a % 2):256 * (a % 2) + 256]
                ts = slice(128 * a, 128 * a + 128)
                if half == 0:
                    PE.do(lambda e, a=a, o=o: e.matmul(o, cT[:, 128 * a:128 * a + 128], be[:, :],
                                                       start=True, stop=False),
                          needs + [("cT", b), ("c", "be")])
                three(o, [((yh[:, k, ts], yl[:, k, ts]), (wouth[:, 2 * half + k, :], woutl[:, 2 * half + k, :]))
                          for k in range(2)],
                      ("O", b, half, a2) if a % 2 else None, needs + ready, start=(half == 1))
            v = acc[:, b % 3, 2 * a2:2 * a2 + 2, :].rearrange("p a c -> p (a c)")
            DV.do(lambda e: e.tensor_tensor(v, P[:, :], v, ALU.add),
                  [("O", b, half, a2)] + grown(b, 2 * a2) + grown(b, 2 * a2 + 1), ("Os", b, half, a2))
            last[(b, 2 * a2)] = last[(b, 2 * a2 + 1)] = ("Os", b, half, a2)
            fill["read"][i] = [("Os", b, half, a2)]

        last = {}

        def grown(b, a):
            return [last.get((b, a), ("ax", b, a))]

        def unit_M(b, n):
            i, P, needs = bank()
            a, e2 = n // 4, n % 4
            ts = slice(128 * a, 128 * a + 128)
            es = slice(512 * e2, 512 * e2 + 512)
            three(P[:, :], [((xTh[:, f, ts], xTl[:, f, ts]), (weh[:, f, es], wel[:, f, es])) for f in range(2)],
                  ("M", b, n), needs + xT_ready(b) + [("wh", f"we{e2}"), ("wl", f"we{e2}")])
            v = acc[:, b % 3, a, :]
            for k in range(2):
                tell = ("Ms", b, n) if k else ("Ms0", b, n)
                DV.do(lambda e, k=k: e.scalar_tensor_tensor(out=v, in0=P[:, 256 * k:256 * k + 256],
                                                            scalar=cpad[:, a, 2 * e2 + k:2 * e2 + k + 1], in1=v,
                                                            op0=ALU.mult, op1=ALU.add),
                      [("M", b, n), ("g", b, "c")] + grown(b, a), tell)
                last[(b, a)] = tell
            fill["read"][i] = [("Ms", b, n)]

        for k in range(2):
            AC.do(lambda e, k=k: e.activation(Pm[:, 0, 16 * k:16 * k + 16], am[:, k, :], ACT.Tanh),
                  [("c", "A"), ("c", "AT")], ("pm", 0) if k else None)

        def krylov(s):
            i, P, needs = bank()
            m = 1 << s
            pw = Pm[:, s % 2, 0:16]
            pt = Pm[:, s % 2, 16:32]
            need = needs + [("pm", s), ("kv", s - 1) if s else ("c", "Bp")]
            PE.do(lambda e: e.matmul(P[0:16, 0:m], pt, V0[:, 0:m], start=True, stop=True), need,
                  ("kx", s) if s == 8 else None)
            if s < 8:
                PE.do(lambda e: e.matmul(P[0:16, 256:272], pt, pw, start=True, stop=True))
                PE.do(lambda e: e.matmul(P[0:16, 272:288], pw, pt, start=True, stop=True), [], ("kx", s))
                DV.do(lambda e: e.tensor_copy(Pm[:, (s + 1) % 2, :], P[0:16, 256:288]), [("kx", s)],
                      ("pm", s + 1))
            DV.do(lambda e: e.tensor_copy(V0[:, m:2 * m], P[0:16, 0:m]), [("kx", s)], ("kv", s))
            fill["read"][i] = [("kv", s)] + ([("pm", s + 1)] if s < 8 else [])

        def response():
            i, P, needs = bank()
            PE.do(lambda e: e.matmul(P[0:1, :], cpc[:, :], V0[:, :], start=True, stop=True),
                  needs + [("kv", 8), ("c", "Cp")], ("kr",))
            DV.do(lambda e: e.tensor_copy(kp[:, 256:768], P[0:1, :]), [("kr",), ("kp0",)], ("kp1",))
            DV.do(lambda e: e.tensor_tensor(kp[:, 256:257], kp[:, 256:257], dpc[:, :], ALU.add),
                  [("kp1",), ("c", "Dp")], ("kp",))
            fill["read"][i] = [("kp1",)]
            dma(SP, kd[:, 0:768], kp, [("kp",)], ("kd",), s_k)
            dma(SP, bass.AP(rd.tensor, 0, [[897, 128], [1, 767]]), bass.AP(kd.tensor, 1, [[0, 128], [1, 767]]),
                [("kd",)], ("rd",), s_k)
            dma(SP, Rraw, rd[:, 127:767], [("rd",)], ("Rraw",), s_k)
            AC.do(lambda e: e.copy(Rh[:, :], Rraw), [("Rraw",)], ("Rh",))
            DV.do(lambda e: e.tensor_tensor(Rl[:, :], Rraw, F(Rh[:, :]), ALU.subtract), [("Rh",)], ("Rl",))

        SR = th[:, :]

        def steps():
            i, P, needs = bank()
            for c, (lo, n, r) in enumerate(((0, 512, 128), (128, 384, 128), (256, 256, 128), (384, 128, 128))):
                PE.do(lambda e, lo=lo, n=n, r=r, c=c: e.matmul(P[:, lo:lo + n], onesf, Rraw[:, r:r + n],
                                                               start=(c == 0), stop=(c == 3)),
                      needs + [("Rraw",), ("ones",)] if c == 0 else [], ("ss",) if c == 3 else None)
            DV.do(lambda e: e.tensor_copy(SR, P[:, :]), [("ss",), ("Rl",)], ("sr",))
            fill["read"][i] = [("sr",)]
            marks.at[("s_ready",)] = marks.at[("sr",)]

        def stack(g):
            r, p = g % 3, 64 * (g % 2)
            b, half = g // 4, (g % 4) // 2
            need = [("qkh", b, half, 0), ("qkh", b, half, 1), ("qkl", b, half, 0), ("qkl", b, half, 1)]
            if g >= 3:
                need += [("ST", 16 * (g - 3) + 15)]
            parts = [(qst, 0, qkh, 0), (qst, 1, qkh, 0), (qst, 2, qkl, 0), (qst, 3, qkl, 0),
                     (kst, 0, qkh, 1), (kst, 1, qkl, 1), (kst, 2, qkh, 1), (kst, 3, qkl, 1)]
            for k, (dst, row, src, w) in enumerate(parts):
                dma(SP, F(dst[16 * row:16 * row + 16, r, :, :]), F(src[p:p + 64, w, :]), need, ("st", g, k), s_st[r])

        def scores(n):
            g, j, a = n // 16, n % 16 // 4, n % 4
            r = g % 3
            P = SB[n % 2]
            need = [("mx", n - 2)] if n >= 2 else []
            if n % 16 == 0:
                need += [("st", g, k) for k in range(8)] + [("qpad",), ("kpad",)]
            PE.do(lambda e: e.matmul(P[:, :], qst[0:96, r, j, 128 * a:128 * a + 128], kst[0:96, r, j, :],
                                     start=True, stop=True), need, ("S", n))
            DV.do(lambda e: e.tensor_reduce(mx[:, g % 2, n % 16:n % 16 + 1], P[:, :], AX.X, ALU.max),
                  [("S", n)] + ([("mt", g - 2)] if g >= 2 and n % 16 == 0 else []), ("mx", n))

        def maxima(g):
            i, P, needs = bank()
            PE.do(lambda e: e.transpose(P[0:16, 0:128], mx[:, g % 2, :], ident[:, :]),
                  needs + [("mx", 16 * g + 15), ("ident",)], ("mt", g))
            free = [("mr", g - 1, 0), ("mr", g - 1, 1)] if g else []
            DV.do(lambda e: e.tensor_copy(mh[:, :], P[0:16, 0:128]), [("mt", g)] + free, ("mh", g))
            DV.do(lambda e: e.tensor_tensor(ml[:, :], P[0:16, 0:128], F(mh[:, :]), ALU.subtract), [("mh", g)],
                  ("ml", g))
            fill["read"][i] = [("ml", g)]
            for k, m in enumerate((mh, ml)):
                dma(SP, F(qst[96 + k:97 + k, g % 3, :, :]), F(m[:, :]), [("ml", g)]
                    + ([("ST", 16 * (g - 3) + 15)] if g >= 3 else []), ("mr", g, k), s_m[g % 3])

        def turned(n):
            g, a, j = n // 16, n % 16 // 4, n % 4
            r = g % 3
            P = TB[n % 2]
            need = [("ex", n - 2)] if n >= 2 else []
            if n % 16 == 0:
                need += [("mr", g, 0), ("mr", g, 1), ("kneg",)]
            PE.do(lambda e: e.matmul(P[:, :], kst[0:98, r, j, 128 * a:128 * a + 128], qst[0:98, r, j, :],
                                     start=True, stop=True), need, ("ST", n))
            AC.do(lambda e: e.activation(Pt[:, n % NP, :], P[:, :], ACT.Exp, scale=0.25),
                  [("ST", n)] + ([("PV", n - NP)] if n >= NP else [("wl", "qk"), ("wl", "vg"), ("wl", "in")]),
                  ("ex", n))

        def values(n):
            g, a, j = n // 16, n % 16 // 4, n % 4
            b, h = g // 4, 4 * (g % 4) + j
            O = OB[g % 2]
            need = [("ex", n)]
            if n % 16 == 0:
                need += [("Vs", b, 3), ("vone",), ("oz", g % 2)] + ([("oc", g - 2)] if g >= 2 else [])
            PE.do(lambda e: e.matmul(O[32 * j:32 * j + 17, :], V[:, b % 2, a, h, :], Pt[:, n % NP, :],
                                     start=(a == 0), stop=(a == 3)), need, ("PV", n))

        def outputs_a(g):
            AC.do(lambda e: e.copy(ot[:, :], OB[g % 2][:, :]),
                  [("PV", 16 * g + 15)] + ([("ox", g - 1)] if g else [("ss",)]), ("oc", g))

        def outputs_b(g):
            b = g // 4
            i, P, needs = bank()
            for a in range(4):
                PE.do(lambda e, a=a: e.transpose(P[:, 128 * a:128 * a + 128], ot[:, 128 * a:128 * a + 128],
                                                 ident[:, :]),
                      needs + [("oc", g)] if a == 0 else [], ("ox", g) if a == 3 else None)
            O4 = P[:, :].rearrange("p (a c) -> p a c", c=32)
            DV.do(lambda e: e.reciprocal(rc[:, :].unsqueeze(2), O4[:, :, 16:17]),
                  [("ox", g)] + ([("an", g - 1)] if g else []), ("rc", g))
            DV.do(lambda e: e.tensor_tensor(at[:, :].rearrange("p (a c) -> p a c", c=16), O4[:, :, 0:16],
                                            rc[:, :].unsqueeze(2).to_broadcast([128, 16, 16]), ALU.mult),
                  [("rc", g)] + ([("ad", g - 1)] if g else []), ("an", g))
            fill["read"][i] = [("an", g)]
            c = 64 * (g % 4)
            v = acc[:, b % 3, :, c:c + 64]
            PO.do(lambda e: e.tensor_tensor(v, v, at[:, :].rearrange("p (a c) -> p a c", a=4), ALU.add),
                  [("an", g)] + [k for a in range(4) for k in grown(b, a)], ("ad", g))
            if g % 4 == 3:
                dma(SP, out[b].rearrange("(a p) d -> p a d", p=128), acc[:, b % 3, :, :],
                    [("ad", g - k) for k in range(4)], ("store", b), s_o)

        plan = {}

        def put(s, order, fn, *args):
            plan.setdefault(s, []).append((order, len(plan[s]) if s in plan else 0, fn, args))

        def units(b, table):
            for s, fn, *args in table:
                put(64 * b + s, 5, fn, b, *args)

        common = [(10, unit_QK, 1, 0), (14, unit_QK, 1, 1), (18, unit_M, 7), (19, unit_M, 8), (21, unit_M, 9),
                  (22, unit_M, 10), (24, unit_M, 11), (25, unit_M, 12), (27, unit_M, 13), (28, unit_M, 14),
                  (30, unit_M, 15)]
        usual = [(-32, unit_T, 0), (-31, unit_T, 1), (-29, unit_Z, 0), (-28, unit_Z, 1), (-25, unit_V, 0),
                 (-24, unit_V, 1), (-23, unit_V, 2), (-22, unit_V, 3), (-21, unit_QK, 0, 0), (-19, unit_QK, 0, 1),
                 (-17, unit_Y, 0), (-15, unit_C), (-14, unit_Y, 1), (-12, unit_M, 0), (-10, unit_M, 1),
                 (-8, unit_M, 2), (-6, unit_O, 0, 0), (-4, unit_O, 0, 1), (-3, unit_M, 3), (-1, unit_Y, 2),
                 (1, unit_M, 4), (3, unit_Y, 3), (5, unit_M, 5), (7, unit_M, 6), (12, unit_O, 1, 0),
                 (16, unit_O, 1, 1)] + common
        first = [(-32, unit_T, 0), (-31, unit_T, 1), (-25, unit_V, 0), (-26, unit_QK, 0, 0), (-27, unit_QK, 0, 1),
                 (-24, unit_V, 1), (-23, unit_V, 2), (-22, unit_V, 3), (2, unit_C), (1, unit_M, 0), (3, unit_M, 1),
                 (4, unit_M, 2), (5, unit_Z, 0), (6, unit_Z, 1), (7, unit_M, 3), (8, unit_Y, 0), (9, unit_M, 4),
                 (11, unit_Y, 1), (13, unit_M, 5), (15, unit_M, 6), (16, unit_O, 0, 0), (17, unit_O, 0, 1),
                 (17, unit_Y, 2), (20, unit_Y, 3), (23, unit_O, 1, 0), (25, unit_O, 1, 1)] + common
        units(0, first)
        for b in range(1, NB):
            units(b, usual)
        for b in range(1, NB):
            put(64 * b - 70 if b > 1 else -10, 0, load_x, b)
            for a in range(4):
                put(64 * b - 46 + a, 6, ln_stats, b, a)
                put(64 * b - 42 + 2 * a, 6, ln_norm, b, a)
        for a in range(4):
            put(-40, 1, ln_stats, 0, a)
        for a in range(4):
            put(-39, 1, ln_norm, 0, a)
        put(-39, 2, split, 0, DV)
        put(-39, 2, split, 1, DV)

        def we3():
            key, stg, src, hi, lo, sc = stages[7]
            dma(SP, stg, kp_rows(src), [("T", 0, 1), ("xl", 0, 3)], ("w", key), s_w[7])

        put(-30, 9, we3)
        for k, n in enumerate((2, 3, 4, 5, 6, 7)):
            put(-20 + k, 3, split, n, DV if n in (5,) else PO)
        for s in range(9):
            put(-33 + s if s < 2 else -33 + s, 7, krylov, s)
        put(-22, 7, response)
        put(-1, 7, steps)
        for d in range(4):
            put(4 + d, 6, bias_tile, d)
        for g in range(NG):
            put(max(16 * g - 11, -11) if g > 1 else (-11 if g == 0 else 0), 1, stack, g)
            put(16 * g + 17, 4, maxima, g)
            put(16 * g + 15 + PV_LAG + 1, 3, outputs_a, g)
            put(16 * g + 15 + PV_LAG + 2, 4, outputs_b, g)
        for n in range(NI):
            put(n, 2, scores, n)
            put(n + ST_LAG, 2, turned, n)
            put(n + PV_LAG, 2, values, n)
        for s in sorted(plan):
            for order, k, fn, args in sorted(plan[s], key=lambda t: t[:2]):
                fn(*args)
        SP.do(lambda e: e.nop(), [("store", NB - 1)])

        block = ctx.enter_context(nc.Block())

        @block.tensor
        def _(e):
            PE.emit(e)

        @block.vector
        def _(e):
            DV.emit(e)

        @block.scalar
        def _(e):
            AC.emit(e)

        @block.gpsimd
        def _(e):
            PO.emit(e)

        @block.sync
        def _(e):
            SP.emit(e)


def kernel(**inputs):
    import numpy as _np
    import concourse.bacc as _bacc
    from concourse import mybir as _mybir
    from concourse.bass_utils import run_bass_kernel_spmd as _run

    t = {k: _np.ascontiguousarray(v) for k, v in inputs.items()}

    def heads(w):
        s = w.shape[:-1]
        return w.reshape(*s, -1, 4, 16).swapaxes(-1, -2).reshape(*s, -1)

    wqkv, bqkv = t["L0_ffn_W_qkv"], t["L0_ffn_b_qkv"]
    lay = {
        "x": t["L0_attn_x"],
        "wqk": heads(wqkv[:, 0:512]),
        "bqk": heads(bqkv[0:512]).reshape(4, 128).T,
        "wvg": _np.concatenate([wqkv[:, 512:768], t["L0_ffn_W_gate"]], axis=1),
        "bv": _np.broadcast_to(bqkv[512:768], (128, 256)),
        "bg": _np.broadcast_to(t["L0_ffn_b_gate"], (128, 8)),
        "win": t["L0_attn_W_in"],
        "bin": t["L0_attn_b_in"].reshape(4, 128).T,
        "cw": t["L0_attn_conv_w"].reshape(4, 128, 4).transpose(1, 0, 2),
        "cb": t["L0_attn_conv_b"].reshape(4, 128).T,
        "A": t["L0_attn_A"],
        "AT": t["L0_attn_A"].T,
        "Bp": t["L0_attn_Bp"],
        "Cp": t["L0_attn_Cp"],
        "Dp": t["L0_attn_Dp"],
        "wout": t["L0_attn_W_out"],
        "bout": _np.broadcast_to(t["L0_attn_b_out"], (128, 256)),
        "wexp": t["L0_ffn_W_experts"].transpose(1, 0, 2).reshape(256, 2048),
        "bexp": t["L0_ffn_b_experts"],
    }
    nc = _bacc.Bacc("TRN2", target_bir_lowering=False, num_devices=1)
    arrays, args = {}, []
    for name, a in lay.items():
        a = _np.ascontiguousarray(a)
        arrays[f"in_{name}"] = a
        args.append(nc.dram_tensor(f"in_{name}", a.shape, _mybir.dt.from_np(a.dtype), kind="ExternalInput").ap())
    o = nc.dram_tensor("out_0", (8, 512, 256), _mybir.dt.float32, kind="ExternalOutput").ap()
    kd = nc.dram_tensor("kd", (1, 768), _mybir.dt.float32, kind="Internal").ap()
    rd = nc.dram_tensor("rd", (128, 896), _mybir.dt.float32, kind="Internal").ap()
    program(nc, *args, o, kd, rd)
    r = _run(nc, [arrays], core_ids=[0])
    return r.results[0]["out_0"]
```

```python
from contextlib import ExitStack

import concourse.bass as bass
from concourse import mybir

F32 = mybir.dt.float32
F32R = mybir.dt.float32r
ALU = mybir.AluOpType
ACT = mybir.ActivationFunctionType
AX = mybir.AxisListType

NB = 8
S = 512
D = 256
NG = 4 * NB
NI = 16 * NG
ST_LAG = 21
NP = 6
GSTEP = 4
RATE0, RATE = 1500, 830
LN_AFTER, LN_FROM = 6, 18
R_WAIT = 8


class Marks:

    def __init__(self):
        self.at = {}

    def name(self, key, sem, value):
        assert key not in self.at, key
        self.at[key] = (sem, value)


class Queue:

    def __init__(self, marks, sem):
        self.marks, self.sem, self.count, self.ops = marks, sem, 0, []
        self.fence, self.latest = [], None

    def known(self, needs):
        for key in needs:
            assert key in self.marks.at, key

    def do(self, fn, needs=(), tell=None):
        needs, self.fence = list(needs) + self.fence, []
        self.known(needs)
        if tell is not None:
            self.count += 1
            self.marks.name(tell, self.sem, self.count)
            self.latest = tell
        self.ops.append((fn, list(needs), self.sem if tell is not None else None, 1))

    def dma(self, fn, needs, tell, sem, counts):
        self.known(needs)
        counts[sem.name] = counts.get(sem.name, 0) + 16
        self.marks.name(tell, sem, counts[sem.name])
        self.ops.append((fn, list(needs), sem, 16))

    def emit(self, eng):
        seen = {}
        for fn, needs, sem, inc in self.ops:
            most = {}
            for key in needs:
                s, v = self.marks.at[key]
                if v > most.get(s.name, (s, 0))[1]:
                    most[s.name] = (s, v)
            for s, v in most.values():
                if seen.get(s.name, 0) < v:
                    eng.wait_ge(s, v)
                    seen[s.name] = v
            ins = fn(eng)
            if sem is not None:
                ins.then_inc(sem, inc)


def program(nc, x, wqk, bqk, wvg, bv, bg, win, bin_, cw, cb, A, AT, Bp, Cp, Dp, wout, bout, wexp, bexp, out, kd, rd):
    ctx = ExitStack()
    with ctx:
        def sb(name, shape, dt=F32):
            return ctx.enter_context(nc.sbuf_tensor(name, shape, dt))

        def sem(name):
            return ctx.enter_context(nc.semaphore(name))

        PS = [ctx.enter_context(nc.psum_tensor(f"PS{i}", [128, 512], F32)) for i in range(8)]
        SB, TB, OB, FB = PS[0:2], PS[2:4], PS[4], PS[5:8]

        qst = sb("qst", [98, 3, 4, 512], F32R)
        kst = sb("kst", [98, 3, 4, 512], F32R)
        Pt = sb("Pt", [128, NP, 512])
        qkh = sb("qkh", [128, 2, 512], F32R)
        qkl = sb("qkl", [128, 2, 512], F32R)
        wqkh = sb("wqkh", [128, 2, 512], F32R)
        wqkl = sb("wqkl", [128, 2, 512], F32R)
        wvh = sb("wvh", [128, 2, 264], F32R)
        wvl = sb("wvl", [128, 2, 264], F32R)
        winh = sb("winh", [128, 2, 512], F32R)
        winl = sb("winl", [128, 2, 512], F32R)
        wouth = sb("wouth", [128, 4, 256], F32R)
        woutl = sb("woutl", [128, 4, 256], F32R)
        weh = sb("weh", [128, 2, 2048], F32R)
        wel = sb("wel", [128, 2, 2048], F32R)
        Rh = sb("Rh", [128, 640], F32R)
        Rl = sb("Rl", [128, 640], F32R)
        Bt = sb("Bt", [128, 4, 512])
        V = sb("V", [128, 2, 4, 16, 17])
        acc = sb("acc", [128, 3, 4, 256])
        xTh = sb("xTh", [128, 2, 512], F32R)
        xTl = sb("xTl", [128, 2, 512], F32R)
        xn = sb("xn", [128, 4, 256])
        xh = sb("xh", [128, 1024], F32R)
        xl = sb("xl", [128, 1024], F32R)
        yh = sb("yh", [128, 2, 512], F32R)
        yl = sb("yl", [128, 2, 512], F32R)
        ys = sb("ys", [128, 2, 512])
        th = sb("th", [128, 512])
        ot = sb("ot", [128, 512])
        ident = sb("ident", [128, 128])
        boutb = sb("boutb", [128, 256])
        bgb = sb("bgb", [128, 8])
        be = sb("be", [8, 256])
        cpad = sb("cpad", [128, 4, 8])
        cT = sb("cT", [8, 512])
        wr = sb("wr", [128, 8])
        mx = sb("mx", [128, 2, 16])
        mh = sb("mh", [16, 128], F32R)
        ml = sb("ml", [16, 128], F32R)
        st6 = sb("st6", [128, 4, 6])
        mv = sb("mv", [128, 4, 2])
        rs = sb("rs", [128, 4])
        ve = sb("ve", [128, 4])
        mhalf = sb("mhalf", [128, 4])
        rc = sb("rc", [128, 16])
        at = sb("at", [128, 256])
        mt = sb("mt", [128, 2, 256])
        bvb = at[:, :]
        bq = sb("bq", [128, 4])
        binc = sb("binc", [128, 4])
        cwc = sb("cwc", [128, 4, 4])
        cbc = sb("cbc", [128, 4])
        bw = sb("bw", [128, 4, 4])
        G = sb("G", [128, 6, 4, 8])
        g4 = sb("g4", [128, 6, 4])
        am = ot[0:16, 128:160].rearrange("p (a c) -> p a c", a=2)
        Pm = ot[0:16, 192:256].rearrange("p (a c) -> p a c", a=2)
        cpc = sb("cpc", [16, 1])
        V0 = th[0:16, :]
        kp = ys[0:1, :, :].rearrange("p a c -> p (a c)")[:, 0:768]
        dpc = sb("dpc", [1, 1])

        xhn = xh[:, :].rearrange("p (a c) -> p a c", a=4)
        xln = xl[:, :].rearrange("p (a c) -> p a c", a=4)
        zh = xh[:, :].rearrange("p (a c) -> p a c", a=2)
        zl = xl[:, :].rearrange("p (a c) -> p a c", a=2)
        Rraw = ys[:, :, :].rearrange("p a c -> p (a c)")[:, 0:640]
        onesf = ot[:, 0:128]

        marks = Marks()
        counts = {}
        PE, DV, AC, PO, SP = (Queue(marks, sem(f"s_{n}")) for n in ("pe", "dve", "act", "pool", "sp"))
        s_w = [sem(f"s_w{i}") for i in range(8)]
        s_c = [sem(f"s_c{i}") for i in range(13)]
        s_x0 = [sem(f"s_x0{i}") for i in range(4)]
        s_x = [sem(f"s_x{i}") for i in range(3)]
        s_st = [sem(f"s_st{i}") for i in range(3)]
        s_m = [sem(f"s_m{i}") for i in range(3)]
        s_k = sem("s_k")
        s_o = sem("s_o")

        def F(ap):
            return ap.bitcast(F32)

        def dma(q, dst, src, needs, tell, s):
            q.dma(lambda e: e.dma_start(dst, src), needs, tell, s, counts)

        def load_x(b, q=SP):
            dma(q, acc[:, b % 3, :, :], x[b].rearrange("(a p) d -> p a d", p=128),
                [("store", b - 3)] if b >= 3 else [[], [("wl", "we2")], [("wl", "out")]][b], ("x", b), s_x[b % 3])

        def kp_rows(w):
            return w.rearrange("(k p) n -> p k n", p=128)

        stages = [
            ("qk", Pt[:, 0:2, :], wqk, wqkh, wqkl, 1.0),
            ("vg", Pt[:, 2:4, :].rearrange("p a c -> p (a c)")[:, 0:528].rearrange("p (k n) -> p k n", k=2),
             wvg, wvh, wvl, 1.0),
            ("we0", Bt[:, 0:2, :], wexp[:, 0:512], weh[:, :, 0:512], wel[:, :, 0:512], 1.0),
            ("we1", Bt[:, 2:4, :], wexp[:, 512:1024], weh[:, :, 512:1024], wel[:, :, 512:1024], 1.0),
            ("in", Pt[:, 4:6, :], win, winh, winl, 1.0),
            ("out", acc[:, 2, :, :], wout, wouth, woutl, 0.5),
            ("we2", acc[:, 1, :, :].rearrange("p a c -> p (a c)").rearrange("p (k n) -> p k n", k=2),
             wexp[:, 1024:1536], weh[:, :, 1024:1536], wel[:, :, 1024:1536], 1.0),
            ("we3", xn[:, :, :].rearrange("p a c -> p (a c)").rearrange("p (k n) -> p k n", k=2),
             wexp[:, 1536:2048], weh[:, :, 1536:2048], wel[:, :, 1536:2048], 1.0),
        ]
        for a in range(4):
            dma(SP, acc[:, 0, a, :], x[0, 128 * a:128 * a + 128, :], [], ("x", 0, a), s_x0[a])
        small = [
            (am[:, 0, :], A), (am[:, 1, :], AT), (V0[:, 0:1], Bp.rearrange("(p o) -> p o", o=1)),
            (cpc[:, :], Cp.rearrange("(p o) -> p o", o=1)), (dpc[:, :], Dp.rearrange("(p o) -> p o", o=1)),
            (bq[:, :], bqk), (bvb, bv), (bgb[:, :], bg),
            (binc[:, :], bin_), (cwc[:, :, :], cw), (cbc[:, :], cb), (boutb[:, :], bout),
        ]
        names = ["A", "AT", "Bp", "Cp", "Dp", "bq", "bv", "bg", "bin", "cw", "cb", "bout"]
        def load_w(n, q):
            dma(q, stages[n][1], kp_rows(stages[n][2]), [], ("w", stages[n][0]), s_w[n])

        def load_c(i, q):
            dma(q, small[i][0], small[i][1], [], ("c", names[i]), s_c[i])

        load_w(0, AC)
        load_w(1, AC)
        load_c(5, SP)
        load_c(7, SP)
        for i in (0, 1, 2, 3, 4, 6, 11):
            load_c(i, SP)
        for n in (2, 3, 4, 6, 5):
            load_w(n, SP)
        for i in range(8, 11):
            load_c(i, SP)
        dma(SP, be[:, :], bexp, [], ("c", "be"), s_c[12])

        PO.do(lambda e: e.memset(mhalf[:, :], -0.5), [], ("mhalf",))
        PO.do(lambda e: e.memset(ident[:, :], 0.0), [], ("id0",))
        PO.do(lambda e: e.affine_select(out=ident[:, :], in_=ident[:, :], compare_op=ALU.not_equal, fill=1.0,
                                        base=0, pattern=[[-1, 128]], channel_multiplier=1),
              [("id0",)], ("ident",))
        PO.do(lambda e: e.memset(F(kst[64:96, 0, :, :]), 0.0), [("ident",)], ("kpad", 0))
        PO.do(lambda e: e.memset(F(kst[96:98, 0, :, :]), -1.0), [("kpad", 0)], ("kneg", 0))
        PO.fence = [("kneg", 0)]
        DV.do(lambda e: e.memset(F(qst[64:96, 0, :, :]), 0.0), [], ("qpad", 0))
        DV.do(lambda e: e.memset(OB[:, :], 0.0), [], ("oz",))

        def constants():
            for k in range(8):
                PO.do(lambda e, k=k: e.memset(wr[:, k:k + 1], float(8 - k)), [], ("wr",) if k == 7 else None)
            PO.do(lambda e: e.memset(V[:, :, :, :, 16:17], 1.0), [], ("vone",))
            PO.do(lambda e: e.memset(onesf, 1.0), [], ("ones",))
            PO.do(lambda e: e.memset(kp, 0.0), [], ("kp0",))

        def pads(r):
            PO.fence = [PO.latest]
            PO.do(lambda e: e.memset(F(qst[64:96, r, :, :]), 0.0), [("vone",), ("ones",), ("kp0",)], ("qpad", r))
            PO.do(lambda e: e.memset(F(kst[64:96, r, :, :]), 0.0), [("qpad", r)], ("kpad", r))
            PO.do(lambda e: e.memset(F(kst[96:98, r, :, :]), -1.0), [("kpad", r)], ("kneg", r))
            PO.fence = [("kneg", r)]

        def split(n, eng):
            key, stg, src, hi, lo, sc = stages[n]
            AC.do(lambda e: e.activation(hi[:, :, :] if key[0:2] != "we" else hi, stg, ACT.Copy, scale=sc),
                  [("w", key)], ("wh", key))
            h = hi[:, :, :] if key[0:2] != "we" else hi
            lw = lo[:, :, :] if key[0:2] != "we" else lo
            if sc != 1.0:
                for a in range(4):
                    eng.do(lambda e, a=a: e.scalar_tensor_tensor(out=lw[:, a, :], in0=stg[:, a, :], scalar=sc,
                                                                 in1=F(h)[:, a, :], op0=ALU.mult,
                                                                 op1=ALU.subtract),
                           [("wh", key)], ("wl", key) if a == 3 else None)
            else:
                eng.do(lambda e: e.tensor_tensor(lw, stg, F(h), ALU.subtract), [("wh", key)], ("wl", key))

        def bias_sum():
            PO.do(lambda e: e.tensor_tensor(boutb[:, :], boutb[:, :], bvb, ALU.add),
                  [("c", "bout"), ("c", "bv")], ("bsum",))

        def ln_stats(b, a):
            xa = acc[:, b % 3, a, :]
            DV.do(lambda e: e.bn_stats(st6[:, a, :], xa), [("x", b) if b else ("x", 0, a)], ("bn", b, a))
            DV.do(lambda e: e.bn_aggr(mv[:, a, :], st6[:, a, :]),
                  [("bn", b, a)] + ([("xn", b - 1, a)] if b else []), ("ag", b, a))
            if a == 3:
                DV.do(lambda e: e.tensor_scalar(ve[:, :], mv[:, :, 1], 1e-5, None, ALU.add),
                      [("ag", b, i) for i in range(4)], ("ve", b))
                PO.do(lambda e: e.tensor_tensor(rs[:, :], ve[:, :], mhalf[:, :], ALU.pow),
                      [("ve", b), ("mhalf",)], ("rs", b))

        def ln_norm(b, a):
            xa = acc[:, b % 3, a, :]
            DV.do(lambda e: e.tensor_scalar(xn[:, a, :], xa, mv[:, a, 0:1], rs[:, a:a + 1],
                                            ALU.subtract, ALU.mult),
                  [("rs", b)] + ([("xl", b - 1, a), ("T", b - 1, 1)] if b else []), ("xn", b, a))
            if b:
                ln_parts(b, a)
                add_bias(b, a)

        def add_bias(b, a):
            xa = acc[:, b % 3, a, :]
            PO.do(lambda e: e.tensor_tensor(xa, xa, boutb[:, :], ALU.add), [("xn", b, a), ("bsum",)],
                  ("ax", b, a))

        def ln_parts(b, a):
            free = [("Y", b - 1, 3)] if b else []
            PO.do(lambda e: e.tensor_copy(xhn[:, a, :], xn[:, a, :]), [("xn", b, a)] + free, ("xh", b, a))
            PO.do(lambda e: e.tensor_tensor(xln[:, a, :], xn[:, a, :], F(xhn[:, a, :]), ALU.subtract),
                  [("xh", b, a)], ("xl", b, a))

        plan = {}
        now = [0]

        def put(s, order, fn, *args):
            plan.setdefault(s, []).append((order, len(plan[s]) if s in plan else 0, fn, args))

        def later(k, order, fn, *args):
            if unit is not None and unit["open"]:
                unit["after"].append((k, order, fn, args))
            else:
                put(now[0] + k, order, fn, *args)

        unit = {"open": False, "ops": [], "after": []}
        todo = []
        credit = [0.0]

        def pe(cost, *args):
            unit["ops"].append((cost, args))

        def pump(cycles):
            credit[0] = min(credit[0] + cycles, cycles)
            while credit[0] > 0:
                if not unit["ops"]:
                    if free_bank() is None:
                        return
                    k = next((k for k, t in enumerate(todo) if t[0](now[0])), None)
                    if k is None:
                        return
                    _, fn, args = todo.pop(k)
                    unit["open"] = True
                    fn(*args)
                    unit["open"] = False
                cost, args = unit["ops"].pop(0)
                PE.do(*args)
                credit[0] -= cost
                if not unit["ops"]:
                    after, unit["after"] = unit["after"], []
                    for k, order, fn, a in after:
                        put(now[0] + k, order, fn, *a)

        fill = {"n": 0, "read": [[], [], []]}

        def free_bank():
            for k in range(3):
                i = (fill["n"] + k) % 3
                if all(r in marks.at for r in fill["read"][i]):
                    return i
            return None

        def bank():
            i = free_bank()
            fill["n"] = i + 1
            needs, fill["read"][i] = fill["read"][i], []
            return i, FB[i], needs

        def three(P, pairs, tell, needs, start=True, stop=True):
            n = 3 * len(pairs)
            k = 0
            for (lh, ll), (rh, rl) in pairs:
                for u, v in ((lh, rh), (ll, rh), (lh, rl)):
                    pe(P.shape[-1], lambda e, u=u, v=v, k=k: e.matmul(P, u, v, start=(start and k == 0),
                                                                      stop=(stop and k == n - 1)),
                       needs if k == 0 else [], tell if k == n - 1 else None)
                    k += 1

        def unit_T(b, f):
            i, P, needs = bank()
            for a in range(4):
                pe(256, lambda e, a=a: e.transpose(P[:, 128 * a:128 * a + 128], xn[:, a, 128 * f:128 * f + 128],
                                                 ident[:, :]),
                      needs + [("xn", b, a), ("ident",)], ("T", b, f) if a == 3 else None)
            free = [("M", b - 1, 15), ("QK", b - 1, 1, 1)] if b else []

            def read():
                AC.do(lambda e: e.copy(xTh[:, f, :], P[:, :]), [("T", b, f)] + free, ("xTh", b, f))
                DV.do(lambda e: e.tensor_tensor(xTl[:, f, :], P[:, :], F(xTh[:, f, :]), ALU.subtract),
                      [("xTh", b, f)], ("xTl", b, f))

            later(1, 1, read)
            fill["read"][i] = [("xTl", b, f)]

        def xT_ready(b):
            return [("xTh", b, 0), ("xTh", b, 1), ("xTl", b, 0), ("xTl", b, 1)]

        def unit_V(b, a):
            i, P, needs = bank()
            ts = slice(128 * a, 128 * a + 128)
            three(P[:, 0:264], [((xTh[:, f, ts], xTl[:, f, ts]), (wvh[:, f, :], wvl[:, f, :])) for f in range(2)],
                  ("V", b, a), needs + xT_ready(b) + [("wh", "vg"), ("wl", "vg")])

            def read():
                AC.do(lambda e: e.copy(V[:, b % 2, a, :, 0:16], P[:, 0:256].rearrange("p (h d) -> p h d", h=16)),
                      [("V", b, a)] + ([("PV", 16 * (b - 2) + 15)] if b >= 2 else []), ("Vs", b, a))
                DV.do(lambda e: e.tensor_tensor(G[:, 0, a, :], P[:, 256:264], bgb[:, :], ALU.add),
                      [("Vs", b, a), ("c", "bg")] + ([("g", b - 1, "c")] if b else []), ("lg", b, a))
                if a == 3:
                    gate(b)

            later(1, 1, read)
            fill["read"][i] = [("lg", b, a)]

        def gate(b):
            def bc(v):
                return v.unsqueeze(2).to_broadcast([128, 4, 8])

            count = [0]

            def stage(q, *args):
                count[0] += 1
                later(1 + count[0] // GSTEP, 3, q.do, *args)

            def step(key, fn, needs):
                stage(DV, fn, [("g", b, k) for k in needs], ("g", b, key))

            stage(DV, lambda e: e.tensor_reduce(g4[:, 0, :], G[:, 0, :, :], AX.X, ALU.max),
                  [("lg", b, a) for a in range(4)], ("g", b, "m"))
            step("s", lambda e: e.tensor_tensor(G[:, 0, :, :], G[:, 0, :, :], bc(g4[:, 0, :]), ALU.subtract), ["m"])
            stage(AC, lambda e: e.activation(G[:, 1, :, :], G[:, 0, :, :], ACT.Exp), [("g", b, "s")], ("g", b, "e"))
            step("z", lambda e: e.tensor_reduce(g4[:, 1, :], G[:, 1, :, :], AX.X, ALU.add), ["e"])
            step("r", lambda e: e.reciprocal(g4[:, 2, :], g4[:, 1, :]), ["z"])
            step("g", lambda e: e.tensor_tensor(G[:, 2, :, :], G[:, 1, :, :], bc(g4[:, 2, :]), ALU.mult), ["r"])
            src, val = 2, "g"
            wrb = wr[:, :].unsqueeze(1).to_broadcast([128, 4, 8])
            for r in range(2):
                step(f"x{r}", lambda e, src=src: e.tensor_reduce(g4[:, 3, :], G[:, src, :, :], AX.X, ALU.max),
                     [val] if r == 0 else [val, "q0"])
                step(f"q{r}", lambda e, src=src: e.tensor_tensor(G[:, 3, :, :], G[:, src, :, :],
                                                                 bc(g4[:, 3, :]), ALU.is_ge),
                     [f"x{r}"] + (["k0"] if r else []))
                stage(DV, lambda e: e.tensor_tensor(G[:, 3, :, :], G[:, 3, :, :], wrb, ALU.mult),
                      [("g", b, f"q{r}"), ("wr",)], ("g", b, f"w{r}"))
                step(f"y{r}", lambda e: e.tensor_reduce(g4[:, 4, :], G[:, 3, :, :], AX.X, ALU.max), [f"w{r}"])
                step(f"k{r}", lambda e, r=r: e.tensor_tensor(G[:, 4 + r, :, :], G[:, 3, :, :], bc(g4[:, 4, :]),
                                                             ALU.is_equal), [f"y{r}"])
                if r == 0:
                    step("d", lambda e: e.scalar_tensor_tensor(out=G[:, 0, :, :], in0=G[:, 4, :, :], scalar=-2.0,
                                                               in1=G[:, 2, :, :], op0=ALU.mult, op1=ALU.add),
                         ["k0"])
                    src, val = 0, "d"
            step("t", lambda e: e.tensor_tensor(G[:, 1, :, :], G[:, 4, :, :], G[:, 5, :, :], ALU.add), ["k1"])
            free = [("M", b - 1, 15), ("g", b - 1, "u"), ("Mc", b - 1, 15, 1)] if b else []
            stage(DV, lambda e: e.tensor_tensor(cpad[:, :, :], G[:, 2, :, :], G[:, 1, :, :], ALU.mult),
                  [("g", b, "t")] + free, ("g", b, "c"))

        def unit_C(b):
            i, P, needs = bank()
            for a in range(4):
                pe(256, lambda e, a=a: e.transpose(P[0:8, 128 * a:128 * a + 128], cpad[:, a, :], ident[:, :]),
                      needs + [("g", b, "c"), ("ident",)] if a == 0 else [], ("g", b, "u") if a == 3 else None)
            later(1, 1, AC.do, lambda e: e.copy(cT[:, :], P[0:8, :]),
                  [("g", b, "u")] + ([("O", b - 1, 0, 1)] if b else []), ("cT", b))
            fill["read"][i] = [("cT", b)]

        def unit_QK(b, half, w):
            i, P, needs = bank()
            m = 2 * w + half
            cs = slice(128 * m, 128 * m + 128)
            three(P[:, :], [((wqkh[:, f, cs], wqkl[:, f, cs]), (xTh[:, f, :], xTl[:, f, :])) for f in range(2)],
                  ("QK", b, half, w), needs + xT_ready(b) + [("wh", "qk"), ("wl", "qk")])
            g = 4 * b + 2 * half
            free = [("st", g - 1, k) for k in range(8)] if g else []

            def read():
                AC.do(lambda e: e.activation(qkh[:, w, :], P[:, :], ACT.Identity, bias=bq[:, m:m + 1]),
                      [("QK", b, half, w), ("c", "bq")] + free, ("qkh", b, half, w))
                later(0, 6, DV.do, lambda e: e.scalar_tensor_tensor(
                    out=qkl[:, w, :], in0=P[:, :], scalar=bq[:, m:m + 1], in1=F(qkh[:, w, :]), op0=ALU.add,
                    op1=ALU.subtract), [("qkh", b, half, w), ("c", "bq")] + free, ("qkl", b, half, w))

            later(1, 1, read)
            fill["read"][i] = [("qkl", b, half, w)]

        def unit_Z(b, f):
            i, P, needs = bank()
            fs = slice(128 * f, 128 * f + 128)
            k = 0
            for c, (lo, n, r) in enumerate(((0, 512, 128), (128, 384, 128), (256, 256, 128), (256, 256, 0))):
                for u, v in ((xhn, Rh), (xln, Rh), (xhn, Rl)):
                    pe(n, lambda e, c=c, lo=lo, n=n, r=r, u=u, v=v, k=k: e.matmul(
                        P[:, lo:lo + n], u[:, c, fs], v[:, r:r + n], start=(k == 0), stop=(k == 11)),
                        needs + [("xh", b, 3), ("xl", b, 3), ("Rh",), ("Rl",)] if k == 0 else [],
                        ("Z", b, f) if k == 11 else None)
                    k += 1
            fill["read"][i] = [("zl", b, f)]
            fill["z", f] = P

            def read(g):
                Q = fill["z", g]
                AC.do(lambda e: e.copy(zh[:, g, :], Q[:, :]), [("Z", b, 0), ("Z", b, 1)], ("zh", b, g))
                DV.do(lambda e: e.tensor_tensor(zl[:, g, :], Q[:, :], F(zh[:, g, :]), ALU.subtract),
                      [("zh", b, g)], ("zl", b, g))

            if f == 1:
                for g in range(2):
                    later(1, 1 + 4 * g, read, g)

        def unit_Y(b, d):
            i, P, needs = bank()
            ds = slice(128 * d, 128 * d + 128)
            three(P[:, :], [((winh[:, f, ds], winl[:, f, ds]), (zh[:, f, :], zl[:, f, :])) for f in range(2)],
                  ("Y", b, d), needs + [("zh", b, 0), ("zh", b, 1), ("zl", b, 0), ("zl", b, 1),
                                        ("wh", "in"), ("wl", "in")])
            y = ys[:, d % 2, :]
            prev = ("y", b, d - 2) if d >= 2 else (("y", b - 1, d + 2) if b else ("ss",))
            later(1, 1, DV.do,
                  lambda e: e.scalar_tensor_tensor(out=y, in0=P[:, :], scalar=cwc[:, d, 3:4], in1=Bt[:, d, :],
                                                   op0=ALU.mult, op1=ALU.add),
                  [("Y", b, d), ("B", d), prev, ("c", "cw")], ("v", b, d, 0))
            for s in (1, 2, 3):
                later(1 + s // 2, 5 if s % 2 else 1, DV.do, lambda e, s=s: e.scalar_tensor_tensor(out=y[:, s:512], in0=P[:, 0:512 - s],
                                                            scalar=cwc[:, d, 3 - s:4 - s], in1=y[:, s:512],
                                                            op0=ALU.mult, op1=ALU.add),
                      [("v", b, d, s - 1)], ("v", b, d, s))
            fill["read"][i] = [("v", b, d, 3)]
            n = 4 * b + d
            last = ("yl", n - 1) if n else None
            later(3, 1, AC.do, lambda e: e.activation(th[:, :], y, ACT.Tanh, scale=0.5),
                  [("v", b, d, 3)] + ([last, ("yh", n - 1)] if last else [("B", k) for k in range(4)]), ("th", b, d))
            later(3, 5, DV.do, lambda e: e.scalar_tensor_tensor(out=th[:, :], in0=th[:, :], scalar=1.0, in1=y,
                                                   op0=ALU.add, op1=ALU.mult), [("th", b, d)], ("y", b, d))
            hb, half = d % 2, d // 2
            free = []
            if half == 1:
                free = [("O", b, 0, 0), ("O", b, 0, 1)]
            elif b:
                free = [("O", b - 1, 1, 0), ("O", b - 1, 1, 1)]
            later(4, 1, AC.do, lambda e: e.copy(yh[:, hb, :], th[:, :]), [("y", b, d)] + free, ("yh", n))
            if d == 3:
                later(5, 7, after_y, b)
            later(4, 5, PO.do, lambda e: e.tensor_tensor(yl[:, hb, :], th[:, :], F(yh[:, hb, :]), ALU.subtract),
                  [("yh", n)] + free, ("yl", n))

        def bias_tile(d):
            sr = SR
            DV.do(lambda e: e.tensor_scalar(bw[:, d, :], cwc[:, d, :], binc[:, d:d + 1], None, ALU.mult),
                  [("c", "cw"), ("c", "bin")], ("bw", d))
            DV.do(lambda e: e.tensor_scalar(Bt[:, d, :], sr, cbc[:, d:d + 1], None, ALU.mult),
                  [("sr",), ("c", "cb"), ("wl", "we0"), ("wl", "we1")], ("B", d, -1))
            for s in range(4):
                DV.do(lambda e, s=s: e.scalar_tensor_tensor(out=Bt[:, d, s:512], in0=sr[:, 0:512 - s],
                                                            scalar=bw[:, d, 3 - s:4 - s], in1=Bt[:, d, s:512],
                                                            op0=ALU.mult, op1=ALU.add),
                      [("bw", d), ("B", d, s - 1)], ("B", d, s) if s < 3 else ("B", d))

        def unit_O(b, half, a2):
            i, P, needs = bank()
            ready = [("yh", 4 * b + 2 * half + k) for k in range(2)] + [("yl", 4 * b + 2 * half + k) for k in range(2)]
            ready += [("wh", "out"), ("wl", "out")]
            for a in (2 * a2, 2 * a2 + 1):
                o = P[:, 256 * (a % 2):256 * (a % 2) + 256]
                ts = slice(128 * a, 128 * a + 128)
                if half == 0:
                    pe(1024, lambda e, a=a, o=o: e.matmul(o, cT[:, 128 * a:128 * a + 128], be[:, :],
                                                       start=True, stop=False),
                          needs + [("cT", b), ("c", "be")])
                three(o, [((yh[:, k, ts], yl[:, k, ts]), (wouth[:, 2 * half + k, :], woutl[:, 2 * half + k, :]))
                          for k in range(2)],
                      ("O", b, half, a2) if a % 2 else None, needs + ready, start=(half == 1))
            v = acc[:, b % 3, 2 * a2:2 * a2 + 2, :].rearrange("p a c -> p (a c)")

            def read():
                DV.do(lambda e: e.tensor_tensor(v, P[:, :], v, ALU.add),
                      [("O", b, half, a2)] + grown(b, 2 * a2) + grown(b, 2 * a2 + 1), ("Os", b, half, a2))
                last[(b, 2 * a2)] = last[(b, 2 * a2 + 1)] = ("Os", b, half, a2)

            later(1, 1, read)
            fill["read"][i] = [("Os", b, half, a2)]

        last = {}

        def grown(b, a):
            return [last.get((b, a), ("ax", b, a))]

        def unit_M(b, n):
            i, P, needs = bank()
            a, e2 = n // 4, n % 4
            ts = slice(128 * a, 128 * a + 128)
            es = slice(512 * e2, 512 * e2 + 512)
            three(P[:, :], [((xTh[:, f, ts], xTl[:, f, ts]), (weh[:, f, es], wel[:, f, es])) for f in range(2)],
                  ("M", b, n), needs + xT_ready(b) + [("wh", f"we{e2}"), ("wl", f"we{e2}")])
            v = acc[:, b % 3, a, :]

            def scale(k):
                free = [("Ms", b, n - 1, k)] if n else ([("Ms", b - 1, 15, k)] if b else [])
                AC.do(lambda e: e.activation(mt[:, k, :], P[:, 256 * k:256 * k + 256], ACT.Copy,
                                             scale=cpad[:, a, 2 * e2 + k:2 * e2 + k + 1]),
                      [("M", b, n), ("g", b, "c")] + free, ("Mc", b, n, k))

            def add(k):
                PO.do(lambda e: e.tensor_tensor(v, v, mt[:, k, :], ALU.add),
                      [("Mc", b, n, k)] + grown(b, a), ("Ms", b, n, k))
                last[(b, a)] = ("Ms", b, n, k)

            for k in range(2):
                later(1, 1 + 4 * k, scale, k)
                later(1, 1 + 4 * k, add, k)
            fill["read"][i] = [("Mc", b, n, 1)]

        def decay():
            for k in range(2):
                AC.do(lambda e, k=k: e.activation(Pm[:, 0, 16 * k:16 * k + 16], am[:, k, :], ACT.Tanh),
                      [("c", "A"), ("c", "AT")], ("pm", 0) if k else None)

        def krylov(s):
            i, P, needs = bank()
            m = 1 << s
            pw = Pm[:, s % 2, 0:16]
            pt = Pm[:, s % 2, 16:32]
            need = needs + [("pm", s), ("kv", s - 1) if s else ("c", "Bp")]
            pe(4 * m, lambda e: e.matmul(P[0:16, 0:m], pt, V0[:, 0:m], start=True, stop=True), need,
               ("kx", s) if s == 8 else None)
            if s < 8:
                pe(256, lambda e: e.matmul(P[0:16, 256:272], pt, pw, start=True, stop=True))
                pe(256, lambda e: e.matmul(P[0:16, 272:288], pw, pt, start=True, stop=True), [], ("kx", s))
                later(0, 7, DV.do, lambda e: e.tensor_copy(Pm[:, (s + 1) % 2, :], P[0:16, 256:288]), [("kx", s)],
                      ("pm", s + 1))
            later(0, 7, DV.do, lambda e: e.tensor_copy(V0[:, m:2 * m], P[0:16, 0:m]), [("kx", s)], ("kv", s))
            fill["read"][i] = [("kv", s)] + ([("pm", s + 1)] if s < 8 else [])

        def response():
            i, P, needs = bank()
            pe(2048, lambda e: e.matmul(P[0:1, :], cpc[:, :], V0[:, :], start=True, stop=True),
               needs + [("kv", 8), ("c", "Cp")], ("kr",))
            fill["read"][i] = [("kp1",)]

            def read():
                DV.do(lambda e: e.tensor_copy(kp[:, 256:768], P[0:1, :]), [("kr",), ("kp0",)], ("kp1",))
                DV.do(lambda e: e.tensor_tensor(kp[:, 256:257], kp[:, 256:257], dpc[:, :], ALU.add),
                      [("kp1",), ("c", "Dp")], ("kp",))
                dma(SP, kd[:, 0:768], kp, [("kp",)], ("kd",), s_k)
                dma(SP, bass.AP(rd.tensor, 0, [[897, 128], [1, 767]]), bass.AP(kd.tensor, 1, [[0, 128], [1, 767]]),
                    [("kd",)], ("rd",), s_k)
                dma(SP, Rraw, rd[:, 127:767], [("rd",)], ("Rraw",), s_k)
                later(R_WAIT, 1, spread)

            later(0, 7, read)

        def spread():
            AC.do(lambda e: e.copy(Rh[:, :], Rraw), [("Rraw",)], ("Rh",))
            DV.do(lambda e: e.tensor_tensor(Rl[:, :], Rraw, F(Rh[:, :]), ALU.subtract), [("Rh",)], ("Rl",))

        SR = th[:, :]

        def steps():
            i, P, needs = bank()
            for c, (lo, n, r) in enumerate(((0, 512, 128), (128, 384, 128), (256, 256, 128), (384, 128, 128))):
                pe(4 * n, lambda e, lo=lo, n=n, r=r, c=c: e.matmul(P[:, lo:lo + n], onesf, Rraw[:, r:r + n],
                                                                   start=(c == 0), stop=(c == 3)),
                   needs + [("Rraw",), ("ones",)] if c == 0 else [], ("ss",) if c == 3 else None)
            later(1, 1, DV.do, lambda e: e.tensor_copy(SR, P[:, :]), [("ss",), ("Rl",)], ("sr",))
            fill["read"][i] = [("sr",)]
            for d in range(4):
                later(2 + d, 6, bias_tile, d)

        def stack(g):
            r, p = g % 3, 64 * (g % 2)
            b, half = g // 4, (g % 4) // 2
            need = [("qkh", b, half, 0), ("qkh", b, half, 1), ("qkl", b, half, 0), ("qkl", b, half, 1)]
            if any(k not in marks.at for k in need):
                return put(now[0] + 1, 1, stack, g)
            if g >= 3:
                need += [("ST", 16 * (g - 3) + 15)]
            parts = [(qst, 0, qkh, 0), (qst, 1, qkh, 0), (qst, 2, qkl, 0), (qst, 3, qkl, 0),
                     (kst, 0, qkh, 1), (kst, 1, qkl, 1), (kst, 2, qkh, 1), (kst, 3, qkl, 1)]
            for k, (dst, row, src, w) in enumerate(parts):
                dma(SP, F(dst[16 * row:16 * row + 16, r, :, :]), F(src[p:p + 64, w, :]), need, ("st", g, k), s_st[r])

        def scores(n):
            g, j, a = n // 16, n % 16 // 4, n % 4
            r = g % 3
            P = SB[n % 2]
            need = [("mx", n - 2)] if n >= 2 else []
            if n % 16 == 0:
                need += [("st", g, k) for k in range(8)] + [("qpad", r), ("kpad", r)]
            PE.do(lambda e: e.matmul(P[:, :], qst[0:96, r, j, 128 * a:128 * a + 128], kst[0:96, r, j, :],
                                     start=True, stop=True), need, ("S", n))
            DV.do(lambda e: e.tensor_reduce(mx[:, g % 2, n % 16:n % 16 + 1], P[:, :], AX.X, ALU.max),
                  [("S", n)] + ([("mt", g - 2)] if g >= 2 and n % 16 == 0 else []), ("mx", n))

        def maxima(g):
            if free_bank() is None:
                return put(now[0] + 1, 4, maxima, g)
            i, P, needs = bank()
            PE.do(lambda e: e.transpose(P[0:16, 0:128], mx[:, g % 2, :], ident[:, :]),
                  needs + [("mx", 16 * g + 15), ("ident",)], ("mt", g))
            free = [("mr", g - 1, 0), ("mr", g - 1, 1)] if g else []
            AC.do(lambda e: e.copy(mh[:, :], P[0:16, 0:128]), [("mt", g)] + free, ("mh", g))
            DV.do(lambda e: e.tensor_tensor(ml[:, :], P[0:16, 0:128], F(mh[:, :]), ALU.subtract), [("mh", g)],
                  ("ml", g))
            fill["read"][i] = [("ml", g)]
            for k, m in enumerate((mh, ml)):
                dma(SP, F(qst[96 + k:97 + k, g % 3, :, :]), F(m[:, :]), [("ml", g)]
                    + ([("ST", 16 * (g - 3) + 15)] if g >= 3 else []), ("mr", g, k), s_m[g % 3])

        def turned(n):
            g, a, j = n // 16, n % 16 // 4, n % 4
            r = g % 3
            P = TB[n % 2]
            need = [("ex", n - 2)] if n >= 2 else []
            if n % 16 == 0:
                need += [("mr", g, 0), ("mr", g, 1), ("kneg", r)]
            PE.do(lambda e: e.matmul(P[:, :], kst[0:98, r, j, 128 * a:128 * a + 128], qst[0:98, r, j, :],
                                     start=True, stop=True), need, ("ST", n))
            AC.do(lambda e: e.activation(Pt[:, n % NP, :], P[:, :], ACT.Exp, scale=0.25),
                  [("ST", n)] + ([("PV", (n - NP) // 4)] if n >= NP else [("wl", "qk"), ("wl", "vg"), ("wl", "in")]),
                  ("ex", n))

        def values(m):
            g, a = m // 4, m % 4
            b = g // 4
            need = [("ex", 4 * m + 3)]
            if a == 0:
                need += [("Vs", b, 3), ("vone",), ("oz",)] + ([("oc", g - 1)] if g else [])
            for j in range(4):
                PE.do(lambda e, j=j: e.matmul(OB[32 * j:32 * j + 17, :], V[:, b % 2, a, 4 * (g % 4) + j, :],
                                              Pt[:, (4 * m + j) % NP, :], start=(a == 0), stop=(a == 3)),
                      need if j == 0 else [], ("PV", m) if j == 3 else None)

        def outputs_a(g):
            AC.do(lambda e: e.copy(ot[:, :], OB[:, :]),
                  [("PV", 4 * g + 3)] + ([("ox", g - 1)] if g else [("ss",)]), ("oc", g))

        def outputs_b(g):
            b = g // 4
            if free_bank() is None:
                return put(now[0] + 1, 5, outputs_b, g)
            i, P, needs = bank()
            for a in range(4):
                PE.do(lambda e, a=a: e.transpose(P[:, 128 * a:128 * a + 128], ot[:, 128 * a:128 * a + 128],
                                                 ident[:, :]),
                      needs + [("oc", g)] if a == 0 else [], ("ox", g) if a == 3 else None)
            O4 = P[:, :].rearrange("p (a c) -> p a c", c=32)
            later(1, 1, DV.do, lambda e: e.reciprocal(rc[:, :].unsqueeze(2), O4[:, :, 16:17]),
                  [("ox", g)] + ([("an", g - 1)] if g else []), ("rc", g))
            later(1, 5, DV.do, lambda e: e.tensor_tensor(at[:, :].rearrange("p (a c) -> p a c", c=16), O4[:, :, 0:16],
                                            rc[:, :].unsqueeze(2).to_broadcast([128, 16, 16]), ALU.mult),
                  [("rc", g)] + ([("ad", g - 1)] if g else [("bsum",)]), ("an", g))
            fill["read"][i] = [("an", g)]
            c = 64 * (g % 4)
            v = acc[:, b % 3, :, c:c + 64]

            def add():
                PO.do(lambda e: e.tensor_tensor(v, v, at[:, :].rearrange("p (a c) -> p a c", a=4), ALU.add),
                      [("an", g)] + [k for a in range(4) for k in grown(b, a)], ("ad", g))
                for a in range(4):
                    last[(b, a)] = ("ad", g)

            later(2, 3, add)
            if g % 4 == 3:
                later(3, 3, dma, SP, out[b].rearrange("(a p) d -> p a d", p=128), acc[:, b % 3, :, :],
                    [("ad", g - k) for k in range(4)], ("store", b), s_o)


        def queued(b, s, *keys):
            return lambda t: t >= 64 * b + s and all(k in marks.at for k in keys)

        def layer_norm(b):
            for a in range(4):
                put(now[0] + a // 2, 6, ln_stats, b, a)
                put(now[0] + 2 + a, 6, ln_norm, b, a)

        def after_y(b):
            if b + 1 < NB:
                put(max(now[0] + LN_AFTER, 64 * b + LN_FROM), 6, layer_norm, b + 1)

        def units(b):
            M = [(queued(b, -64, ("g", b, "c"), ("wl", f"we{n % 4}"), *([("M", b, n - 1)] if n else [])), unit_M, (b, n)) for n in range(16)]
            T = [(queued(b, -40, ("xn", b, 3), *([("M", b - 1, n) for n in range(16)] + [("QK", b - 1, 1, 1)] if b else [])), unit_T, (b, f)) for f in range(2)]
            Z = [(queued(b, -64, ("xl", b, 3), ("Rl",)), unit_Z, (b, f)) for f in range(2)]
            v = [(queued(b, -64, ("xTl", b, 1)), unit_V, (b, a)) for a in range(4)]
            qk0 = [(queued(b, -64, ("xTl", b, 1), *([("st", 4 * b - 1, 7)] if b else [])), unit_QK, (b, 0, w))
                   for w in range(2)]
            Y = [(queued(b, -64, ("zl", b, 1), ("B", 3), *([("y", b, d - 1)] if d else []), *([("O", b, 0, 1)] if d == 2 else [("O", b - 1, 1, 1)] if b and d == 0 else [])), unit_Y, (b, d)) for d in range(4)]
            C = [(queued(b, -64, ("g", b, "c")), unit_C, (b,))]
            O = [(queued(b, -64, ("cT", b), ("yl", 4 * b + 2 * h + 1)), unit_O, (b, h, a))
                 for h in range(2) for a in range(2)]
            qk1 = [(queued(b, 6, ("st", 4 * b + 1, 7)), unit_QK, (b, 1, w)) for w in range(2)]
            if b == 0:
                K = [(queued(0, -64, ("pm", s), *([("kv", s - 1)] if s else [])), krylov, (s,)) for s in range(9)]
                K += [(queued(0, -64, ("kv", 8)), response, ()), (queued(0, -64, ("Rl",)), steps, ())]
                return (T + qk0 + qk1 + v[0:1] + K[0:1] + v[1:2] + K[1:2] + v[2:3] + K[2:3] + v[3:4] + K[3:4] + M[0:1] + K[4:5]
                        + C + K[5:6] + M[1:2] + K[6:7] + M[2:3] + K[7:8] + M[3:4] + K[8:9] + M[4:5] + K[9:10] + M[5:7]
                        + K[10:] + Z + [Y[0]]
                        + M[7:9] + [Y[1]] + M[9:11] + [Y[2]] + O[0:2] + [Y[3]] + M[11:14] + O[2:4] + M[14:])
            return (T + Z + v + qk0 + qk1 + [Y[0]] + M[0:1] + C + M[1:2] + [Y[1]] + M[2:4] + O[0:2] + [Y[2]] + M[4:6]
                    + [Y[3]] + M[6:8] + O[2:4] + M[8:])

        for b in range(NB):
            todo += units(b)
        for b in range(1, NB):
            put(64 * b - 70 if b > 1 else 0, 0, load_x, b)
        for a in range(4):
            put(-40, 1, ln_stats, 0, a)
        put(-40, 2, constants)
        put(-39, 0, split, 0, DV)
        for a in range(4):
            put(-39, 1, ln_norm, 0, a)
        put(-38, 1, bias_sum)
        put(-31, 2, decay)
        put(-30, 2, split, 1, DV)
        put(-8, 2, pads, 1)
        put(4, 2, pads, 2)
        for a in range(4):
            put(-37, 1, add_bias, 0, a)
            put(-14 + a, 4, ln_parts, 0, a)

        def we3():
            key, stg, src, hi, lo, sc = stages[7]
            dma(SP, stg, kp_rows(src), [("T", 0, 1), ("xl", 0, 3)], ("w", key), s_w[7])

        put(-10, 9, we3)
        for k, n in enumerate((2, 3, 4, 5, 6, 7)):
            put(-22 + 2 * k if k < 2 else 2 * k - 14, 3, split, n, DV if n in (5,) else PO)
        for g in range(NG):
            put(max(16 * g - 11, -11) if g > 1 else (-11 if g == 0 else 0), 1, stack, g)
            put(16 * g + 17, 4, maxima, g)
            put(16 * g + ST_LAG + 18, 0, outputs_a, g)
            put(16 * g + ST_LAG + 19, 5, outputs_b, g)
        for n in range(NI):
            put(n, 2, scores, n)
            put(n + ST_LAG, 4, turned, n)
        for m in range(NI // 4):
            put(4 * m + ST_LAG + 5, 5, values, m)
        for s in range(-32, 0):
            put(s, 3, pump, 3000)
        for s in range(0, NI + 60):
            for order in (3, 5):
                put(s, order, pump, RATE0 if s < ST_LAG else RATE)
        while plan:
            now[0] = min(plan)
            for order, k, fn, args in sorted(plan.pop(now[0]), key=lambda t: t[:2]):
                fn(*args)
        SP.do(lambda e: e.nop(), [("store", NB - 1)])

        block = ctx.enter_context(nc.Block())

        @block.tensor
        def _(e):
            PE.emit(e)

        @block.vector
        def _(e):
            DV.emit(e)

        @block.scalar
        def _(e):
            AC.emit(e)

        @block.gpsimd
        def _(e):
            PO.emit(e)

        @block.sync
        def _(e):
            SP.emit(e)


def kernel(**inputs):
    import numpy as _np
    import concourse.bacc as _bacc
    from concourse import mybir as _mybir
    from concourse.bass_utils import run_bass_kernel_spmd as _run

    t = {k: _np.ascontiguousarray(v) for k, v in inputs.items()}

    def heads(w):
        s = w.shape[:-1]
        return w.reshape(*s, -1, 4, 16).swapaxes(-1, -2).reshape(*s, -1)

    wqkv, bqkv = t["L0_ffn_W_qkv"], t["L0_ffn_b_qkv"]
    lay = {
        "x": t["L0_attn_x"],
        "wqk": heads(wqkv[:, 0:512]),
        "bqk": heads(bqkv[0:512]).reshape(4, 128).T,
        "wvg": _np.concatenate([wqkv[:, 512:768], t["L0_ffn_W_gate"]], axis=1),
        "bv": _np.broadcast_to(bqkv[512:768], (128, 256)),
        "bg": _np.broadcast_to(t["L0_ffn_b_gate"], (128, 8)),
        "win": t["L0_attn_W_in"],
        "bin": t["L0_attn_b_in"].reshape(4, 128).T,
        "cw": t["L0_attn_conv_w"].reshape(4, 128, 4).transpose(1, 0, 2),
        "cb": t["L0_attn_conv_b"].reshape(4, 128).T,
        "A": t["L0_attn_A"],
        "AT": t["L0_attn_A"].T,
        "Bp": t["L0_attn_Bp"],
        "Cp": t["L0_attn_Cp"],
        "Dp": t["L0_attn_Dp"],
        "wout": t["L0_attn_W_out"],
        "bout": _np.broadcast_to(t["L0_attn_b_out"], (128, 256)),
        "wexp": t["L0_ffn_W_experts"].transpose(1, 0, 2).reshape(256, 2048),
        "bexp": t["L0_ffn_b_experts"],
    }
    nc = _bacc.Bacc("TRN2", target_bir_lowering=False, num_devices=1)
    arrays, args = {}, []
    for name, a in lay.items():
        a = _np.ascontiguousarray(a)
        arrays[f"in_{name}"] = a
        args.append(nc.dram_tensor(f"in_{name}", a.shape, _mybir.dt.from_np(a.dtype), kind="ExternalInput").ap())
    o = nc.dram_tensor("out_0", (8, 512, 256), _mybir.dt.float32, kind="ExternalOutput").ap()
    kd = nc.dram_tensor("kd", (1, 768), _mybir.dt.float32, kind="Internal").ap()
    rd = nc.dram_tensor("rd", (128, 896), _mybir.dt.float32, kind="Internal").ap()
    program(nc, *args, o, kd, rd)
    r = _run(nc, [arrays], core_ids=[0])
    return r.results[0]["out_0"]
```

```python
from contextlib import ExitStack

import concourse.bass as bass
from concourse import mybir

F32 = mybir.dt.float32
F32R = mybir.dt.float32r
ALU = mybir.AluOpType
ACT = mybir.ActivationFunctionType
AX = mybir.AxisListType

NB = 8
S = 512
D = 256
NG = 4 * NB
NI = 16 * NG

ST_LAG = 21
NP = 6
NM = 2
GATE_POOL = ('c', 'g', 'h', 's', 't', 'w0', 'w1')
O_POOL = (0, 1, 3)
XN_POOL = ()
OFF = -12000
GSTEP = 2
AHEAD = 33
END = 515
POOL_SPLITS = (3,)
B_WAIT = 4
ORDER = "RTTZMRZVoVMMVVQCMQYOYOYMYMMMMMMMMOMMM"
ORDER0 = "QTKRVQMKVRSMKTKMKVCMKZKKYKKBMZBMYBBMVMYMMMOOYMMMMOM"
YLAG = (7, 16, 21, 26, 33, 33, 47, 47)
MLAG = (6, 6, 11, 15)
ZLAG = (15, 13)
QLAG = 6
VLAG = 7
TLAG = 13
OLAG = 7
RLAG = 13
GLAG = (6, 7, 30)
SPLITS = (22, 23, 40, 41, 32, 36)
PARTS = 18
TURN = 425
MOST = 1300
BATCH = 105000
LN_AFTER = 0
LN_FROM = 18
LN_GAP = 1
R_WAIT = 11
START = -38
PAD1 = 16


class Marks:

    def __init__(self):
        self.at = {}

    def name(self, key, sem, value):
        assert key not in self.at, key
        self.at[key] = (sem, value)


class Queue:

    def __init__(self, marks, sem):
        self.marks, self.sem, self.count, self.ops = marks, sem, 0, []
        self.fence, self.latest = [], None

    def known(self, needs):
        for key in needs:
            assert key in self.marks.at, key

    def do(self, fn, needs=(), tell=None):
        needs, self.fence = list(needs) + self.fence, []
        self.known(needs)
        if tell is not None:
            self.count += 1
            self.marks.name(tell, self.sem, self.count)
            self.latest = tell
        self.ops.append((fn, list(needs), self.sem if tell is not None else None, 1))

    def dma(self, fn, needs, tell, sem, counts):
        self.known(needs)
        counts[sem.name] = counts.get(sem.name, 0) + 16
        self.marks.name(tell, sem, counts[sem.name])
        self.ops.append((fn, list(needs), sem, 16))

    def emit(self, eng):
        seen = {}
        for fn, needs, sem, inc in self.ops:
            most = {}
            for key in needs:
                s, v = self.marks.at[key]
                if v > most.get(s.name, (s, 0))[1]:
                    most[s.name] = (s, v)
            for s, v in most.values():
                if seen.get(s.name, 0) < v:
                    eng.wait_ge(s, v)
                    seen[s.name] = v
            ins = fn(eng)
            if sem is not None:
                ins.then_inc(sem, inc)


def program(nc, x, wqk, bqk, wvg, bv, bg, win, bin_, cw, cwt, cb, A, AT, Bp, Cp, Dp, wout, bout, wexp, bexp, out, kd, rd):
    ctx = ExitStack()
    with ctx:
        def sb(name, shape, dt=F32):
            return ctx.enter_context(nc.sbuf_tensor(name, shape, dt))

        def sem(name):
            return ctx.enter_context(nc.semaphore(name))

        PS = [ctx.enter_context(nc.psum_tensor(f"PS{i}", [128, 512], F32)) for i in range(8)]
        SB, TB, OB, FB = PS[0:2], PS[2:4], PS[4], PS[5:8]

        qst = sb("qst", [98, 3, 4, 512], F32R)
        kst = sb("kst", [98, 3, 4, 512], F32R)
        Pt = sb("Pt", [128, NP, 512])
        qkh = sb("qkh", [128, 2, 512], F32R)
        qkl = sb("qkl", [128, 2, 512], F32R)
        wqkh = sb("wqkh", [128, 2, 512], F32R)
        wqkl = sb("wqkl", [128, 2, 512], F32R)
        wvh = sb("wvh", [128, 2, 264], F32R)
        wvl = sb("wvl", [128, 2, 264], F32R)
        winh = sb("winh", [128, 2, 512], F32R)
        winl = sb("winl", [128, 2, 512], F32R)
        wouth = sb("wouth", [128, 4, 256], F32R)
        woutl = sb("woutl", [128, 4, 256], F32R)
        weh = sb("weh", [128, 2, 2048], F32R)
        wel = sb("wel", [128, 2, 2048], F32R)
        Rh = sb("Rh", [128, 640], F32R)
        Rl = sb("Rl", [128, 640], F32R)
        Bt = sb("Bt", [128, 4, 512])
        V = sb("V", [128, 2, 4, 16, 17])
        acc = sb("acc", [128, 3, 4, 256])
        xTh = sb("xTh", [128, 2, 512], F32R)
        xTl = sb("xTl", [128, 2, 512], F32R)
        xn = sb("xn", [128, 4, 256])
        xh = sb("xh", [128, 1024], F32R)
        xl = sb("xl", [128, 1024], F32R)
        yh = sb("yh", [128, 2, 512], F32R)
        yl = sb("yl", [128, 2, 512], F32R)
        ys = sb("ys", [128, 2, 512])
        th = sb("th", [128, 512])
        ot = sb("ot", [128, 512])
        ident = sb("ident", [128, 128])
        bgb = sb("bgb", [128, 8])
        be = sb("be", [28, 256], F32R)
        cpad = sb("cpad", [128, 4, 8])
        cT = sb("cT", [28, 512], F32R)
        cst = sb("cst", [128, 4, 28], F32R)
        braw = Pt[32:42, 2, 0:256]
        bhi = Pt[32:42, 3, 0:256].bitcast(F32R)
        blo = Pt[32:42, 3, 256:512].bitcast(F32R)
        wr = sb("wr", [128, 8])
        mx = sb("mx", [128, 2, 16])
        mh = sb("mh", [16, 128], F32R)
        ml = sb("ml", [16, 128], F32R)
        st6 = sb("st6", [128, 4, 6])
        mv = sb("mv", [128, 4, 2])
        rs = sb("rs", [128, 4])
        ve = sb("ve", [128, 4])
        mhalf = sb("mhalf", [128, 4])
        rc = sb("rc", [128, 16])
        at = sb("at", [128, 256])
        mt = sb("mt", [128, NM, 256])
        bq = sb("bq", [128, 4])
        cwc = sb("cwc", [128, 4, 4])
        srow = Pt[0:1, 0:2, :].rearrange("p a c -> p (a c)")
        bwr = Pt[0:5, 2, :]
        binr = Pt[0:4, 3, :]
        srs = th[0:5, :]
        G = sb("G", [128, 6, 4, 8])
        g4 = sb("g4", [128, 6, 4])
        am = ot[0:16, 128:160].rearrange("p (a c) -> p a c", a=2)
        Pm = ot[0:16, 192:256].rearrange("p (a c) -> p a c", a=2)
        cpc = sb("cpc", [16, 1])
        V0 = th[0:16, :]
        kp = ys[0:1, :, :].rearrange("p a c -> p (a c)")[:, 0:768]
        dpc = sb("dpc", [1, 1])

        xhn = xh[:, :].rearrange("p (a c) -> p a c", a=4)
        xln = xl[:, :].rearrange("p (a c) -> p a c", a=4)
        zh = xh[:, :].rearrange("p (a c) -> p a c", a=2)
        zl = xl[:, :].rearrange("p (a c) -> p a c", a=2)
        Rraw = ys[:, :, :].rearrange("p a c -> p (a c)")[:, 0:640]
        onesf = ot[:, 0:1]

        marks = Marks()
        counts = {}
        PE, DV, AC, PO, SP = (Queue(marks, sem(f"s_{n}")) for n in ("pe", "dve", "act", "pool", "sp"))
        s_w = [sem(f"s_w{i}") for i in range(8)]
        s_c = [sem(f"s_c{i}") for i in range(8)]
        s_x0 = [sem(f"s_x0{i}") for i in range(4)]
        s_x = [sem(f"s_x{i}") for i in range(3)]
        s_st = [sem(f"s_st{i}") for i in range(3)]
        s_m = [sem(f"s_m{i}") for i in range(3)]
        s_k = sem("s_k")
        s_b = sem("s_b")
        s_e = sem("s_e")
        s_o = sem("s_o")

        def F(ap):
            return ap.bitcast(F32)

        def dma(q, dst, src, needs, tell, s):
            q.dma(lambda e: e.dma_start(dst, src), needs, tell, s, counts)

        def load_x(b, q=SP):
            if b >= 3 and ("store", b - 3) not in marks.at:
                return put(now[0] + 1, 0, load_x, b)
            dma(q, acc[:, b % 3, :, :], x[b].rearrange("(a p) d -> p a d", p=128),
                [("store", b - 3)] if b >= 3 else [[], [("wl", "we2")], [("wl", "out")]][b], ("x", b), s_x[b % 3])

        def kp_rows(w):
            return w.rearrange("(k p) n -> p k n", p=128)

        stages = [
            ("qk", Pt[:, 0:2, :], wqk, wqkh, wqkl, 1.0),
            ("vg", Pt[:, 2:4, :].rearrange("p a c -> p (a c)")[:, 0:528].rearrange("p (k n) -> p k n", k=2),
             wvg, wvh, wvl, 1.0),
            ("we0", Bt[:, 0:2, :], wexp[:, 0:512], weh[:, :, 0:512], wel[:, :, 0:512], 1.0),
            ("we1", Bt[:, 2:4, :], wexp[:, 512:1024], weh[:, :, 512:1024], wel[:, :, 512:1024], 1.0),
            ("in", Pt[:, 4:6, :], win, winh, winl, 1.0),
            ("out", acc[:, 2, :, :], wout, wouth, woutl, 0.5),
            ("we2", acc[:, 1, :, :].rearrange("p a c -> p (a c)").rearrange("p (k n) -> p k n", k=2),
             wexp[:, 1024:1536], weh[:, :, 1024:1536], wel[:, :, 1024:1536], 1.0),
            ("we3", xn[:, :, :].rearrange("p a c -> p (a c)").rearrange("p (k n) -> p k n", k=2),
             wexp[:, 1536:2048], weh[:, :, 1536:2048], wel[:, :, 1536:2048], 1.0),
        ]
        for a in range(4):
            dma(SP, acc[:, 0, a, :], x[0, 128 * a:128 * a + 128, :], [], ("x", 0, a), s_x0[a])
        small = [
            (am[:, 0, :], A), (am[:, 1, :], AT), (V0[:, 0:1], Bp.rearrange("(p o) -> p o", o=1)),
            (cpc[:, :], Cp.rearrange("(p o) -> p o", o=1)), (dpc[:, :], Dp.rearrange("(p o) -> p o", o=1)),
            (bq[:, :], bqk), (bgb[:, :], bg),
            (cwc[:, :, :], cw),
        ]
        names = ["A", "AT", "Bp", "Cp", "Dp", "bq", "bg", "cw"]
        def load_w(n, q):
            dma(q, stages[n][1], kp_rows(stages[n][2]), [], ("w", stages[n][0]), s_w[n])

        def load_c(i, q):
            dma(q, small[i][0], small[i][1], [], ("c", names[i]), s_c[i])

        load_w(0, AC)
        load_w(1, AC)
        load_c(5, SP)
        load_c(6, SP)
        for i in range(5):
            load_c(i, SP)
        for n in (2, 3, 4, 6, 5):
            load_w(n, SP)
        load_c(7, SP)

        PO.do(lambda e: e.memset(mhalf[:, :], -0.5), [], ("mhalf",))
        PO.do(lambda e: e.memset(ident[:, :], 0.0), [], ("id0",))
        PO.do(lambda e: e.affine_select(out=ident[:, :], in_=ident[:, :], compare_op=ALU.not_equal, fill=1.0,
                                        base=0, pattern=[[-1, 128]], channel_multiplier=1),
              [("id0",)], ("ident",))
        PO.do(lambda e: e.memset(F(kst[64:96, 0, :, :]), 0.0), [("ident",)], ("kpad", 0))
        PO.do(lambda e: e.memset(F(kst[96:98, 0, :, :]), -1.0), [("kpad", 0)], ("kneg", 0))
        PO.fence = [("kneg", 0)]
        DV.do(lambda e: e.memset(F(qst[64:96, 0, :, :]), 0.0), [], ("qpad", 0))
        DV.do(lambda e: e.memset(OB[:, :], 0.0), [], ("oz",))
        DV.do(lambda e: e.memset(F(cst[:, :, :]), 1.0), [], ("cst1",))

        def constants():
            for k in range(8):
                PO.do(lambda e, k=k: e.memset(wr[:, k:k + 1], float(8 - k)), [], ("wr",) if k == 7 else None)
            PO.do(lambda e: e.memset(V[:, :, :, :, 16:17], 1.0), [], ("vone",))
            PO.do(lambda e: e.memset(onesf, 1.0), [], ("ones",))
            PO.do(lambda e: e.memset(kp, 0.0), [], ("kp0",))

        def pads(r):
            PO.fence = [PO.latest]
            PO.do(lambda e: e.memset(F(qst[64:96, r, :, :]), 0.0), [("vone",), ("ones",), ("kp0",)], ("qpad", r))
            PO.do(lambda e: e.memset(F(kst[64:96, r, :, :]), 0.0), [("qpad", r)], ("kpad", r))
            PO.do(lambda e: e.memset(F(kst[96:98, r, :, :]), -1.0), [("kpad", r)], ("kneg", r))
            PO.fence = [("kneg", r)]

        def split(n, eng):
            key, stg, src, hi, lo, sc = stages[n]
            AC.do(lambda e: e.activation(hi[:, :, :] if key[0:2] != "we" else hi, stg, ACT.Copy, scale=sc),
                  [("w", key)], ("wh", key))
            h = hi[:, :, :] if key[0:2] != "we" else hi
            lw = lo[:, :, :] if key[0:2] != "we" else lo
            if sc != 1.0:
                for a in range(4):
                    eng.do(lambda e, a=a: e.scalar_tensor_tensor(out=lw[:, a, :], in0=stg[:, a, :], scalar=sc,
                                                                 in1=F(h)[:, a, :], op0=ALU.mult,
                                                                 op1=ALU.subtract),
                           [("wh", key)], ("wl", key) if a == 3 else None)
            else:
                eng.do(lambda e: e.tensor_tensor(lw, stg, F(h), ALU.subtract), [("wh", key)], ("wl", key))

        def ln_stats(b, a):
            xa = acc[:, b % 3, a, :]
            DV.do(lambda e: e.bn_stats(st6[:, a, :], xa), [("x", b) if b else ("x", 0, a)], ("bn", b, a))
            DV.do(lambda e: e.bn_aggr(mv[:, a, :], st6[:, a, :]),
                  [("bn", b, a)] + ([("xn", b - 1, a)] if b else []), ("ag", b, a))
            if a == 3:
                DV.do(lambda e: e.tensor_scalar(ve[:, :], mv[:, :, 1], 1e-5, None, ALU.add),
                      [("ag", b, i) for i in range(4)], ("ve", b))
                PO.do(lambda e: e.tensor_tensor(rs[:, :], ve[:, :], mhalf[:, :], ALU.pow),
                      [("ve", b), ("mhalf",)], ("rs", b))

        def ln_norm(b, a):
            xa = acc[:, b % 3, a, :]
            q = PO if b and a in XN_POOL else DV
            q.do(lambda e: e.tensor_scalar(xn[:, a, :], xa, mv[:, a, 0:1], rs[:, a:a + 1],
                                            ALU.subtract, ALU.mult),
                  [("rs", b)] + ([("xl", b - 1, a), ("T", b - 1, 1)] if b else []), ("xn", b, a))
            if b:
                later(0, 6, ln_parts, b, a)

        def ln_parts(b, a):
            free = [("Y", b - 1, 3)] if b else []
            AC.do(lambda e: e.copy(xhn[:, a, :], xn[:, a, :]), [("xn", b, a)] + free, ("xh", b, a))
            PO.do(lambda e: e.tensor_tensor(xln[:, a, :], xn[:, a, :], F(xhn[:, a, :]), ALU.subtract),
                  [("xh", b, a)], ("xl", b, a))

        plan = {}
        now = [0]

        def put(s, order, fn, *args):
            plan.setdefault(s, []).append((order, len(plan[s]) if s in plan else 0, fn, args))

        def later(k, order, fn, *args):
            if unit is not None and unit["open"]:
                unit["after"].append((k, order, fn, args))
            else:
                put(now[0] + k, order, fn, *args)

        def soon(lag, fn, *args):
            later(lag // 10, lag % 10, fn, *args)

        unit = {"open": False, "ops": [], "after": []}
        todo = []
        credit = [0.0]
        spent = [OFF]

        def pe(cost, *args):
            unit["ops"].append((cost, args))

        def pace(half):
            s = now[0] + 0.5 * half
            goal = BATCH * (min(s, TURN) + AHEAD) / 64
            if s > TURN:
                goal += (BATCH * NB - goal) * (s - TURN) / (END - TURN)
            return max(0, min(goal - spent[0], MOST))

        def pump(half, cycles=None):
            credit[0] = min(credit[0], 0) + cycles if cycles else pace(half)
            while credit[0] > 0:
                if not unit["ops"]:
                    if free_bank() is None:
                        return
                    k = next((k for k, t in enumerate(todo) if t[0](now[0])), None)
                    if k is None:
                        return
                    _, fn, args = todo.pop(k)
                    unit["open"] = True
                    fn(*args)
                    unit["open"] = False
                cost, args = unit["ops"].pop(0)
                PE.do(*args)
                credit[0] -= cost
                spent[0] += cost
                if not unit["ops"]:
                    after, unit["after"] = unit["after"], []
                    for k, order, fn, a in after:
                        put(now[0] + k, order, fn, *a)

        fill = {"n": 0, "read": [[], [], []]}

        def free_bank():
            for k in range(3):
                i = (fill["n"] + k) % 3
                if all(r in marks.at for r in fill["read"][i]):
                    return i
            return None

        def bank():
            i = free_bank()
            fill["n"] = i + 1
            needs, fill["read"][i] = fill["read"][i], []
            return i, FB[i], needs

        def three(P, pairs, tell, needs, start=True, stop=True):
            n = 3 * len(pairs)
            k = 0
            for (lh, ll), (rh, rl) in pairs:
                for u, v in ((lh, rh), (ll, rh), (lh, rl)):
                    pe(P.shape[-1], lambda e, u=u, v=v, k=k: e.matmul(P, u, v, start=(start and k == 0),
                                                                      stop=(stop and k == n - 1)),
                       needs if k == 0 else [], tell if k == n - 1 else None)
                    k += 1

        def unit_T(b, f):
            i, P, needs = bank()
            for a in range(4):
                pe(256, lambda e, a=a: e.transpose(P[:, 128 * a:128 * a + 128], xn[:, a, 128 * f:128 * f + 128],
                                                 ident[:, :]),
                      needs + [("xn", b, a), ("ident",)], ("T", b, f) if a == 3 else None)
            free = [("M", b - 1, 15), ("QK", b - 1, 1, 1)] if b else []

            def read():
                AC.do(lambda e: e.copy(xTh[:, f, :], P[:, :]), [("T", b, f)] + free, ("xTh", b, f))
                DV.do(lambda e: e.tensor_tensor(xTl[:, f, :], P[:, :], F(xTh[:, f, :]), ALU.subtract),
                      [("xTh", b, f)], ("xTl", b, f))

            soon(TLAG, read)
            fill["read"][i] = [("xTl", b, f)]

        def xT_ready(b):
            return [("xTh", b, 0), ("xTh", b, 1), ("xTl", b, 0), ("xTl", b, 1)]

        def unit_V(b, a):
            i, P, needs = bank()
            ts = slice(128 * a, 128 * a + 128)
            three(P[:, 0:264], [((xTh[:, f, ts], xTl[:, f, ts]), (wvh[:, f, :], wvl[:, f, :])) for f in range(2)],
                  ("V", b, a), needs + xT_ready(b) + [("wh", "vg"), ("wl", "vg")])

            def read():
                AC.do(lambda e: e.copy(V[:, b % 2, a, :, 0:16], P[:, 0:256].rearrange("p (h d) -> p h d", h=16)),
                      [("V", b, a)] + ([("PV", 16 * (b - 2) + 15)] if b >= 2 else []), ("Vs", b, a))
                DV.do(lambda e: e.tensor_tensor(G[:, 0, a, :], P[:, 256:264], bgb[:, :], ALU.add),
                      [("Vs", b, a), ("c", "bg")] + ([("g", b - 1, "c")] if b else []), ("lg", b, a))
                if a == 3:
                    gate(b)

            soon(VLAG, read)
            fill["read"][i] = [("lg", b, a)]

        def gate(b):
            def bc(v):
                return v.unsqueeze(2).to_broadcast([128, 4, 8])

            count = [0]

            def stage(q, *args):
                count[0] += 1
                later(1 + count[0] // GSTEP, 3, q.do, *args)

            def on(key):
                return PO if key in GATE_POOL else DV

            def step(key, fn, needs):
                stage(on(key), fn, [("g", b, k) for k in needs], ("g", b, key))

            stage(DV, lambda e: e.tensor_reduce(g4[:, 0, :], G[:, 0, :, :], AX.X, ALU.max),
                  [("lg", b, a) for a in range(4)], ("g", b, "m"))
            step("s", lambda e: e.tensor_tensor(G[:, 0, :, :], G[:, 0, :, :], bc(g4[:, 0, :]), ALU.subtract), ["m"])
            stage(AC, lambda e: e.activation(G[:, 1, :, :], G[:, 0, :, :], ACT.Exp), [("g", b, "s")], ("g", b, "e"))
            step("z", lambda e: e.tensor_reduce(g4[:, 1, :], G[:, 1, :, :], AX.X, ALU.add), ["e"])
            step("r", lambda e: e.reciprocal(g4[:, 2, :], g4[:, 1, :]), ["z"])
            step("g", lambda e: e.tensor_tensor(G[:, 2, :, :], G[:, 1, :, :], bc(g4[:, 2, :]), ALU.mult), ["r"])
            src, val = 2, "g"
            wrb = wr[:, :].unsqueeze(1).to_broadcast([128, 4, 8])
            for r in range(2):
                step(f"x{r}", lambda e, src=src: e.tensor_reduce(g4[:, 3, :], G[:, src, :, :], AX.X, ALU.max),
                     [val] if r == 0 else [val, "q0"])
                step(f"q{r}", lambda e, src=src: e.tensor_tensor(G[:, 3, :, :], G[:, src, :, :],
                                                                 bc(g4[:, 3, :]), ALU.is_ge),
                     [f"x{r}"] + (["k0"] if r else []))
                stage(on(f"w{r}"), lambda e: e.tensor_tensor(G[:, 3, :, :], G[:, 3, :, :], wrb, ALU.mult),
                      [("g", b, f"q{r}"), ("wr",)], ("g", b, f"w{r}"))
                step(f"y{r}", lambda e: e.tensor_reduce(g4[:, 4, :], G[:, 3, :, :], AX.X, ALU.max), [f"w{r}"])
                step(f"k{r}", lambda e, r=r: e.tensor_tensor(G[:, 4 + r, :, :], G[:, 3, :, :], bc(g4[:, 4, :]),
                                                             ALU.is_equal), [f"y{r}"])
                if r == 0:
                    step("d", lambda e: e.scalar_tensor_tensor(out=G[:, 0, :, :], in0=G[:, 4, :, :], scalar=-2.0,
                                                               in1=G[:, 2, :, :], op0=ALU.mult, op1=ALU.add),
                         ["k0"])
                    src, val = 0, "d"
            step("t", lambda e: e.tensor_tensor(G[:, 1, :, :], G[:, 4, :, :], G[:, 5, :, :], ALU.add), ["k1"])
            free = [("M", b - 1, 15), ("g", b - 1, "u"), ("Mc", b - 1, 15, 1)] if b else []
            stage(on("c"), lambda e: e.tensor_tensor(cpad[:, :, :], G[:, 2, :, :], G[:, 1, :, :], ALU.mult),
                  [("g", b, "t")] + free, ("g", b, "c"))
            c2 = cst[:, :, 0:20].rearrange("p a (r c) -> p a r c", r=2)
            for r in range(2):
                stage(on("h"), lambda e, r=r: e.tensor_copy(c2[:, :, r, 0:8], cpad[:, :, :]), [("g", b, "c")],
                      ("g", b, f"h{r}"))
            stage(on("l"), lambda e: e.tensor_tensor(cst[:, :, 20:28], cpad[:, :, :], F(cst[:, :, 0:8]), ALU.subtract),
                  [("g", b, "h0"), ("g", b, "h1"), ("cst1",)], ("g", b, "l"))

        def unit_C(b):
            i, P, needs = bank()
            for a in range(4):
                pe(256, lambda e, a=a: e.transpose(P[0:28, 128 * a:128 * a + 128], F(cst[:, a, :]), ident[:, :]),
                   needs + [("g", b, "l"), ("ident",)] if a == 0 else [], ("g", b, "u") if a == 3 else None)
            later(1, 1, AC.do, lambda e: e.copy(cT[:, :], P[0:28, :]),
                  [("g", b, "u")] + ([("O", b - 1, 0, 1)] if b else []), ("cT", b))
            fill["read"][i] = [("cT", b)]

        def unit_QK(b, half, w):
            i, P, needs = bank()
            m = 2 * w + half
            cs = slice(128 * m, 128 * m + 128)
            three(P[:, :], [((wqkh[:, f, cs], wqkl[:, f, cs]), (xTh[:, f, :], xTl[:, f, :])) for f in range(2)],
                  ("QK", b, half, w), needs + xT_ready(b) + [("wh", "qk"), ("wl", "qk")])
            g = 4 * b + 2 * half
            free = [("st", g - 1, k) for k in range(8)] if g else []

            def read():
                AC.do(lambda e: e.activation(qkh[:, w, :], P[:, :], ACT.Identity, bias=bq[:, m:m + 1]),
                      [("QK", b, half, w), ("c", "bq")] + free, ("qkh", b, half, w))
                soon(QLAG, DV.do, lambda e: e.scalar_tensor_tensor(
                    out=qkl[:, w, :], in0=P[:, :], scalar=bq[:, m:m + 1], in1=F(qkh[:, w, :]), op0=ALU.add,
                    op1=ALU.subtract), [("qkh", b, half, w), ("c", "bq")] + free, ("qkl", b, half, w))

            soon(RLAG, read)
            fill["read"][i] = [("qkl", b, half, w)]

        def unit_Z(b, f):
            i, P, needs = bank()
            fs = slice(128 * f, 128 * f + 128)
            k = 0
            for c, (lo, n, r) in enumerate(((0, 512, 128), (128, 384, 128), (256, 256, 128), (256, 256, 0))):
                for u, v in ((xhn, Rh), (xln, Rh), (xhn, Rl)):
                    pe(n, lambda e, c=c, lo=lo, n=n, r=r, u=u, v=v, k=k: e.matmul(
                        P[:, lo:lo + n], u[:, c, fs], v[:, r:r + n], start=(k == 0), stop=(k == 11)),
                        needs + [("xh", b, 3), ("xl", b, 3), ("Rh",), ("Rl",)] if k == 0 else [],
                        ("Z", b, f) if k == 11 else None)
                    k += 1
            fill["read"][i] = [("zl", b, f)]
            fill["z", f] = P

            def read(g):
                Q = fill["z", g]
                AC.do(lambda e: e.copy(zh[:, g, :], Q[:, :]), [("Z", b, 0), ("Z", b, 1)], ("zh", b, g))
                DV.do(lambda e: e.tensor_tensor(zl[:, g, :], Q[:, :], F(zh[:, g, :]), ALU.subtract),
                      [("zh", b, g)], ("zl", b, g))

            if f == 1:
                for g in range(2):
                    soon(ZLAG[g], read, g)

        def unit_Y(b, d):
            i, P, needs = bank()
            ds = slice(128 * d, 128 * d + 128)
            three(P[:, :], [((winh[:, f, ds], winl[:, f, ds]), (zh[:, f, :], zl[:, f, :])) for f in range(2)],
                  ("Y", b, d), needs + [("zh", b, 0), ("zh", b, 1), ("zl", b, 0), ("zl", b, 1),
                                        ("wh", "in"), ("wl", "in")])
            y = ys[:, d % 2, :]
            prev = ("y", b, d - 2) if d >= 2 else (("y", b - 1, d + 2) if b else ("ss",))
            soon(YLAG[0], DV.do,
                  lambda e: e.scalar_tensor_tensor(out=y, in0=P[:, :], scalar=cwc[:, d, 3:4], in1=Bt[:, d, :],
                                                   op0=ALU.mult, op1=ALU.add),
                  [("Y", b, d), ("B", d), prev, ("c", "cw")], ("v", b, d, 0))
            for s in (1, 2, 3):
                soon(YLAG[s], DV.do, lambda e, s=s: e.scalar_tensor_tensor(out=y[:, s:512], in0=P[:, 0:512 - s],
                                                            scalar=cwc[:, d, 3 - s:4 - s], in1=y[:, s:512],
                                                            op0=ALU.mult, op1=ALU.add),
                      [("v", b, d, s - 1)], ("v", b, d, s))
            fill["read"][i] = [("v", b, d, 3)]
            n = 4 * b + d
            last = ("yl", n - 1) if n else None
            soon(YLAG[4], AC.do, lambda e: e.activation(th[:, :], y, ACT.Tanh, scale=0.5),
                  [("v", b, d, 3)] + ([last, ("yh", n - 1)] if last else [("B", k) for k in range(4)]), ("th", b, d))
            soon(YLAG[5], DV.do, lambda e: e.scalar_tensor_tensor(out=th[:, :], in0=th[:, :], scalar=1.0, in1=y,
                                                   op0=ALU.add, op1=ALU.mult), [("th", b, d)], ("y", b, d))
            hb, half = d % 2, d // 2
            free = []
            if half == 1:
                free = [("O", b, 0, 0), ("O", b, 0, 1)]
            elif b:
                free = [("O", b - 1, 1, 0), ("O", b - 1, 1, 1)]
            soon(YLAG[6], AC.do, lambda e: e.copy(yh[:, hb, :], th[:, :]), [("y", b, d)] + free, ("yh", n))
            if d == 3:
                later(YLAG[7] // 10 + 1, 7, after_y, b)
            soon(YLAG[7], PO.do, lambda e: e.tensor_tensor(yl[:, hb, :], th[:, :], F(yh[:, hb, :]), ALU.subtract),
                  [("yh", n)] + free, ("yl", n))

        def bias_rows():
            dma(SP, bwr[0:4, :], cwt, [("wl", "vg")], ("bt", 0), s_b)
            dma(SP, bwr[4:5, :], cb, [("wl", "vg")], ("bt", 1), s_b)
            dma(SP, binr, bin_, [("wl", "vg")], ("bt", 2), s_b)
            DV.do(lambda e: e.memset(srow[:, 0:3], 0.0), [("wl", "qk")], ("sr0",))
            DV.do(lambda e: e.tensor_tensor(bwr[0:4, :], bwr[0:4, :], binr, ALU.mult), [("bt", k) for k in range(3)],
                  ("bwr",))

        def bias_split():
            for k, (rows, src) in enumerate(((slice(32, 40), bexp), (slice(40, 41), bout), (slice(41, 42), bv))):
                dma(SP, Pt[rows, 2, 0:256], src, [("wl", "vg")], ("br", k), s_e)
            AC.do(lambda e: e.copy(bhi, braw), [("br", k) for k in range(3)], ("bh",))
            DV.do(lambda e: e.tensor_tensor(blo, braw, F(bhi), ALU.subtract), [("bh",)], ("bl",))
            for k, (rows, src) in enumerate(((slice(0, 10), bhi), (slice(10, 20), blo), (slice(20, 28), bhi[0:8, :]))):
                dma(SP, F(be[rows, :]), F(src), [("bl",)], ("be", k), s_e)

        def unit_B(d):
            i, P, needs = bank()
            pe(2048, lambda e: e.matmul(P[:, :], bwr[:, 128 * d:128 * d + 128], srs, start=True, stop=True),
               needs + [("srs", k) for k in range(5)] + [("bwr",)], ("Bm", d))
            later(1, 1, AC.do, lambda e: e.copy(Bt[:, d, :], P[:, :]), [("Bm", d), ("wl", "we0"), ("wl", "we1")],
                  ("B", d))
            fill["read"][i] = [("B", d)]

        def unit_O(b, half, a2):
            i, P, needs = bank()
            ready = [("yh", 4 * b + 2 * half + k) for k in range(2)] + [("yl", 4 * b + 2 * half + k) for k in range(2)]
            ready += [("wh", "out"), ("wl", "out")]
            for a in (2 * a2, 2 * a2 + 1):
                o = P[:, 256 * (a % 2):256 * (a % 2) + 256]
                ts = slice(128 * a, 128 * a + 128)
                if half == 0:
                    pe(256, lambda e, a=a, o=o: e.matmul(o, cT[:, 128 * a:128 * a + 128], be[:, :],
                                                       start=True, stop=False),
                          needs + [("cT", b)] + [("be", k) for k in range(3)])
                three(o, [((yh[:, k, ts], yl[:, k, ts]), (wouth[:, 2 * half + k, :], woutl[:, 2 * half + k, :]))
                          for k in range(2)],
                      ("O", b, half, a2) if a % 2 else None, needs + ready, start=(half == 1))
            v = acc[:, b % 3, 2 * a2:2 * a2 + 2, :].rearrange("p a c -> p (a c)")

            def read():
                DV.do(lambda e: e.tensor_tensor(v, P[:, :], v, ALU.add),
                      [("O", b, half, a2)] + grown(b, 2 * a2) + grown(b, 2 * a2 + 1), ("Os", b, half, a2))
                last[(b, 2 * a2)] = last[(b, 2 * a2 + 1)] = ("Os", b, half, a2)

            def copy(k):
                u = turn_mt(("Os", b, half, a2, k) if k == 0 else ("Os", b, half, a2))
                AC.do(lambda e: e.copy(mt[:, u % NM, :], P[:, 256 * k:256 * k + 256]),
                      [("O", b, half, a2)] + mt_free(u), ("Oc", b, half, a2, k))
                w = acc[:, b % 3, 2 * a2 + k, :]
                tell = readers[u]
                PO.do(lambda e: e.tensor_tensor(w, w, mt[:, u % NM, :], ALU.add),
                      [("Oc", b, half, a2, k)] + grown(b, 2 * a2 + k), tell)
                last[(b, 2 * a2 + k)] = tell

            if 2 * half + a2 in O_POOL:
                soon(OLAG, copy, 0)
                soon(OLAG + 4, copy, 1)
                fill["read"][i] = [("Oc", b, half, a2, 1)]
            else:
                soon(OLAG, read)
                fill["read"][i] = [("Os", b, half, a2)]

        last = {}

        def grown(b, a):
            return [last.get((b, a), ("xn", b, a))]

        slot, readers = {}, []

        def turn_mt(key):
            readers.append(key)
            return len(readers) - 1

        def mt_free(u):
            return [readers[u - NM]] if u >= NM else []

        def unit_M(b, n):
            i, P, needs = bank()
            a, e2 = n // 4, n % 4
            ts = slice(128 * a, 128 * a + 128)
            es = slice(512 * e2, 512 * e2 + 512)
            three(P[:, :], [((xTh[:, f, ts], xTl[:, f, ts]), (weh[:, f, es], wel[:, f, es])) for f in range(2)],
                  ("M", b, n), needs + xT_ready(b) + [("wh", f"we{e2}"), ("wl", f"we{e2}")])
            v = acc[:, b % 3, a, :]

            def scale(k):
                u = turn_mt(("Ms", b, n, k))
                free = mt_free(u)
                slot[n, k] = u % NM
                AC.do(lambda e: e.activation(mt[:, u % NM, :], P[:, 256 * k:256 * k + 256], ACT.Copy,
                                             scale=cpad[:, a, 2 * e2 + k:2 * e2 + k + 1]),
                      [("M", b, n), ("g", b, "c")] + free, ("Mc", b, n, k))

            def add(k):
                i = slot[n, k]
                PO.do(lambda e: e.tensor_tensor(v, v, mt[:, i, :], ALU.add),
                      [("Mc", b, n, k)] + grown(b, a), ("Ms", b, n, k))
                last[(b, a)] = ("Ms", b, n, k)

            for k in range(2):
                soon(MLAG[2 * k], scale, k)
                soon(MLAG[2 * k + 1], add, k)
            fill["read"][i] = [("Mc", b, n, 1)]

        def decay():
            for k in range(2):
                AC.do(lambda e, k=k: e.activation(Pm[:, 0, 16 * k:16 * k + 16], am[:, k, :], ACT.Tanh),
                      [("c", "A"), ("c", "AT")], ("pm", 0) if k else None)

        def krylov(s):
            i, P, needs = bank()
            m = 1 << s
            pw = Pm[:, s % 2, 0:16]
            pt = Pm[:, s % 2, 16:32]
            need = needs + [("pm", s), ("kv", s - 1) if s else ("c", "Bp")]
            pe(4 * m, lambda e: e.matmul(P[0:16, 0:m], pt, V0[:, 0:m], start=True, stop=True), need,
               ("kx", s) if s == 8 else None)
            if s < 8:
                pe(256, lambda e: e.matmul(P[0:16, 256:272], pt, pw, start=True, stop=True))
                pe(256, lambda e: e.matmul(P[0:16, 272:288], pw, pt, start=True, stop=True), [], ("kx", s))
                later(0, 7, DV.do, lambda e: e.tensor_copy(Pm[:, (s + 1) % 2, :], P[0:16, 256:288]), [("kx", s)],
                      ("pm", s + 1))
            later(0, 7, DV.do, lambda e: e.tensor_copy(V0[:, m:2 * m], P[0:16, 0:m]), [("kx", s)], ("kv", s))
            fill["read"][i] = [("kv", s)] + ([("pm", s + 1)] if s < 8 else [])

        def response():
            i, P, needs = bank()
            pe(2048, lambda e: e.matmul(P[0:1, :], cpc[:, :], V0[:, :], start=True, stop=True),
               needs + [("kv", 8), ("c", "Cp")], ("kr",))
            fill["read"][i] = [("kp1",)]

            def read():
                DV.do(lambda e: e.tensor_copy(kp[:, 256:768], P[0:1, :]), [("kr",), ("kp0",)], ("kp1",))
                DV.do(lambda e: e.tensor_tensor(kp[:, 256:257], kp[:, 256:257], dpc[:, :], ALU.add),
                      [("kp1",), ("c", "Dp")], ("kp",))
                dma(SP, kd[:, 0:768], kp, [("kp",)], ("kd",), s_k)
                dma(SP, bass.AP(rd.tensor, 0, [[897, 128], [1, 767]]), bass.AP(kd.tensor, 1, [[0, 128], [1, 767]]),
                    [("kd",)], ("rd",), s_k)
                dma(SP, Rraw, rd[:, 127:767], [("rd",)], ("Rraw",), s_k)
                later(R_WAIT, 1, spread)

            later(0, 7, read)

        def spread():
            AC.do(lambda e: e.copy(Rh[:, :], Rraw), [("Rraw",)], ("Rh",))
            DV.do(lambda e: e.tensor_tensor(Rl[:, :], Rraw, F(Rh[:, :]), ALU.subtract), [("Rh",)], ("Rl",))

        due = set()

        def steps():
            i, P, needs = bank()
            for c, (lo, n, r) in enumerate(((0, 512, 128), (128, 384, 128), (256, 256, 128), (384, 128, 128))):
                pe(4 * n, lambda e, lo=lo, n=n, r=r, c=c: e.matmul(P[0:1, lo:lo + n], onesf, Rraw[:, r:r + n],
                                                                   start=(c == 0), stop=(c == 3)),
                   needs + [("Rraw",), ("ones",)] if c == 0 else [], ("ss",) if c == 3 else None)

            def read():
                DV.do(lambda e: e.tensor_copy(srow[:, 3:515], P[0:1, :]), [("ss",), ("sr0",)], ("sr",))
                for k, shift in enumerate((0, 1, 2, 3, 3)):
                    dma(SP, srs[k:k + 1, :], srow[:, shift:shift + 512], [("sr",), ("kr",)], ("srs", k), s_b)
                later(B_WAIT, 1, due.add, "B")

            later(1, 1, read)
            fill["read"][i] = [("sr",)]

        def stack(g):
            r, p = g % 3, 64 * (g % 2)
            b, half = g // 4, (g % 4) // 2
            need = [("qkh", b, half, 0), ("qkh", b, half, 1), ("qkl", b, half, 0), ("qkl", b, half, 1)]
            if any(k not in marks.at for k in need):
                return put(now[0] + 1, 1, stack, g)
            if g >= 3:
                need += [("ST", 16 * (g - 3) + 15)]
            parts = [(qst, 0, qkh, 0), (qst, 1, qkh, 0), (qst, 2, qkl, 0), (qst, 3, qkl, 0),
                     (kst, 0, qkh, 1), (kst, 1, qkl, 1), (kst, 2, qkh, 1), (kst, 3, qkl, 1)]
            for k, (dst, row, src, w) in enumerate(parts):
                dma(SP, F(dst[16 * row:16 * row + 16, r, :, :]), F(src[p:p + 64, w, :]), need, ("st", g, k), s_st[r])

        def scores(n):
            g, j, a = n // 16, n % 16 // 4, n % 4
            r = g % 3
            P = SB[n % 2]
            need = [("mx", n - 2)] if n >= 2 else []
            if n % 16 == 0:
                need += [("st", g, k) for k in range(8)] + [("qpad", r), ("kpad", r)]
            PE.do(lambda e: e.matmul(P[:, :], qst[0:96, r, j, 128 * a:128 * a + 128], kst[0:96, r, j, :],
                                     start=True, stop=True), need, ("S", n))
            DV.do(lambda e: e.tensor_reduce(mx[:, g % 2, n % 16:n % 16 + 1], P[:, :], AX.X, ALU.max),
                  [("S", n)] + ([("mt", g - 2)] if g >= 2 and n % 16 == 0 else []), ("mx", n))

        def maxima(g):
            if free_bank() is None:
                return put(now[0] + 1, 4, maxima, g)
            i, P, needs = bank()
            PE.do(lambda e: e.transpose(P[0:16, 0:128], mx[:, g % 2, :], ident[:, :]),
                  needs + [("mx", 16 * g + 15), ("ident",)], ("mt", g))
            free = [("mr", g - 1, 0), ("mr", g - 1, 1)] if g else []
            AC.do(lambda e: e.copy(mh[:, :], P[0:16, 0:128]), [("mt", g)] + free, ("mh", g))
            DV.do(lambda e: e.tensor_tensor(ml[:, :], P[0:16, 0:128], F(mh[:, :]), ALU.subtract), [("mh", g)],
                  ("ml", g))
            fill["read"][i] = [("ml", g)]
            for k, m in enumerate((mh, ml)):
                dma(SP, F(qst[96 + k:97 + k, g % 3, :, :]), F(m[:, :]), [("ml", g)]
                    + ([("ST", 16 * (g - 3) + 15)] if g >= 3 else []), ("mr", g, k), s_m[g % 3])

        def turned(n):
            g, a, j = n // 16, n % 16 // 4, n % 4
            r = g % 3
            P = TB[n % 2]
            need = [("ex", n - 2)] if n >= 2 else []
            if n % 16 == 0:
                need += [("mr", g, 0), ("mr", g, 1), ("kneg", r)]
            PE.do(lambda e: e.matmul(P[:, :], kst[0:98, r, j, 128 * a:128 * a + 128], qst[0:98, r, j, :],
                                     start=True, stop=True), need, ("ST", n))
            AC.do(lambda e: e.activation(Pt[:, n % NP, :], P[:, :], ACT.Exp, scale=0.25),
                  [("ST", n)] + ([("PV", (n - NP) // 4)] if n >= NP else [("Bm", 3), ("srs", 4), ("wl", "in")] + [("be", k) for k in range(3)]),
                  ("ex", n))

        def values(m):
            g, a = m // 4, m % 4
            b = g // 4
            need = [("ex", 4 * m + 3)]
            if a == 0:
                need += [("Vs", b, 3), ("vone",), ("oz",)] + ([("oc", g - 1)] if g else [])
            for j in range(4):
                PE.do(lambda e, j=j: e.matmul(OB[32 * j:32 * j + 17, :], V[:, b % 2, a, 4 * (g % 4) + j, :],
                                              Pt[:, (4 * m + j) % NP, :], start=(a == 0), stop=(a == 3)),
                      need if j == 0 else [], ("PV", m) if j == 3 else None)

        def outputs_a(g):
            AC.do(lambda e: e.copy(ot[:, :], OB[:, :]),
                  [("PV", 4 * g + 3)] + ([("ox", g - 1)] if g else [("ss",)]), ("oc", g))

        def outputs_b(g):
            b = g // 4
            if free_bank() is None:
                return put(now[0] + 1, 5, outputs_b, g)
            i, P, needs = bank()
            for a in range(4):
                PE.do(lambda e, a=a: e.transpose(P[:, 128 * a:128 * a + 128], ot[:, 128 * a:128 * a + 128],
                                                 ident[:, :]),
                      needs + [("oc", g)] if a == 0 else [], ("ox", g) if a == 3 else None)
            O4 = P[:, :].rearrange("p (a c) -> p a c", c=32)
            soon(GLAG[0], DV.do, lambda e: e.reciprocal(rc[:, :].unsqueeze(2), O4[:, :, 16:17]),
                  [("ox", g)] + ([("an", g - 1)] if g else []), ("rc", g))
            soon(GLAG[1], DV.do, lambda e: e.tensor_tensor(at[:, :].rearrange("p (a c) -> p a c", c=16), O4[:, :, 0:16],
                                            rc[:, :].unsqueeze(2).to_broadcast([128, 16, 16]), ALU.mult),
                  [("rc", g)] + ([("ad", g - 1)] if g else []), ("an", g))
            fill["read"][i] = [("an", g)]
            c = 64 * (g % 4)
            v = acc[:, b % 3, :, c:c + 64]

            def add():
                PO.do(lambda e: e.tensor_tensor(v, v, at[:, :].rearrange("p (a c) -> p a c", a=4), ALU.add),
                      [("an", g)] + [k for a in range(4) for k in grown(b, a)], ("ad", g))
                for a in range(4):
                    last[(b, a)] = ("ad", g)

            soon(GLAG[2], add)
            if g % 4 == 3:
                later(GLAG[2] // 10 + 1, 3, store, b)

        def store(b):
            if any(k not in marks.at for k in (("ad", 4 * b + 3), ("Ms", b, 15, 1), ("Os", b, 1, 1))):
                return put(now[0] + 1, 3, store, b)
            dma(SP, out[b].rearrange("(a p) d -> p a d", p=128), acc[:, b % 3, :, :],
                [k for a in range(4) for k in grown(b, a)], ("store", b), s_o)


        def queued(b, s, *keys):
            return lambda t: t >= 64 * b + s and all(k in marks.at for k in keys)

        def layer_norm(b):
            for a in range(4):
                put(now[0] + a // 2, 6, ln_stats, b, a)
                put(now[0] + 2 + LN_GAP * a, 6, ln_norm, b, a)

        def after_y(b):
            if b + 1 < NB:
                put(max(now[0] + LN_AFTER, 64 * b + LN_FROM), 6, layer_norm, b + 1)

        held = []

        def units(b):
            M = [(queued(b, -64, ("g", b, "c"), ("wl", f"we{n % 4}"), *([("M", b, n - 1)] if n else [])), unit_M, (b, n)) for n in range(16)]
            T = [(queued(b, -40, ("xn", b, 3), *([("M", b - 1, n) for n in range(16)] + [("QK", b - 1, 1, 1)] if b else [])), unit_T, (b, f)) for f in range(2)]
            Z = [(queued(b, -64, ("xl", b, 3), ("Rl",)), unit_Z, (b, f)) for f in range(2)]
            v = [(queued(b, -64, ("xTl", b, 1)), unit_V, (b, a)) for a in range(4)]
            qk0 = [(queued(b, -64, ("xTl", b, 1), *([("st", 4 * b - 1, 7)] if b else [])), unit_QK, (b, 0, w))
                   for w in range(2)]
            Y = [(queued(b, -64, ("zl", b, 1), ("B", 3), *([("y", b, d - 1)] if d else []), *([("O", b, 0, 1)] if d == 2 else [("O", b - 1, 1, 1)] if b and d == 0 else [])), unit_Y, (b, d)) for d in range(4)]
            C = [(queued(b, -64, ("g", b, "l")), unit_C, (b,))]
            O = [(queued(b, -64, ("cT", b), ("yl", 4 * b + 2 * h + 1)), unit_O, (b, h, a))
                 for h in range(2) for a in range(2)]
            qk1 = [(queued(b, 6 if b else -64, ("st", 4 * b + 1, 7)), unit_QK, (b, 1, w)) for w in range(2)]
            K = [(queued(0, -64, ("pm", s), *([("kv", s - 1)] if s else [])), krylov, (s,)) for s in range(9)]
            K += [(queued(0, -64, ("kv", 8)), response, ())]
            kinds = {"T": T, "Z": Z, "V": v, "Q": qk0, "R": qk1, "Y": Y, "M": M, "C": C, "O": held, "K": K,
                     "S": [(queued(0, -64, ("Rl",)), steps, ())],
                     "B": [(lambda t: "B" in due, unit_B, (d,)) for d in range(4)]}
            kinds["o"], held[:] = list(held), O
            taken = [kinds[c].pop(0) for c in (ORDER if b else ORDER0)]
            assert not kinds["o"]
            return taken + (held if b == NB - 1 else [])

        for b in range(NB):
            todo += units(b)
        for b in range(1, NB):
            put(64 * b - 70 if b > 1 else max(START + 40, 0), 0, load_x, b)
        for a in range(4):
            put(START, 1, ln_stats, 0, a)
        put(START, 2, constants)
        put(START + 1, 0, split, 0, DV)
        for a in range(4):
            put(START + 1, 1, ln_norm, 0, a)
        put(START + 9, 2, decay)
        put(START + 10, 2, split, 1, DV)
        put(START + 14, 6, bias_rows)
        put(START + 15, 7, bias_split)
        put(START + PAD1, 2, pads, 1)
        put(START + PAD1 + 12, 2, pads, 2)
        for a in range(4):
            put(START + PARTS + a, 4, ln_parts, 0, a)

        def we3():
            key, stg, src, hi, lo, sc = stages[7]
            dma(SP, stg, kp_rows(src), [("T", 0, 1), ("xl", 0, 3)], ("w", key), s_w[7])

        put(START + 30, 9, we3)
        for k, n in enumerate((2, 3, 4, 5, 6, 7)):
            put(START + SPLITS[k], 3, split, n, PO if n in POOL_SPLITS else DV)
        for g in range(NG):
            put(max(16 * g - 11, START + 10), 1, stack, g)
            put(16 * g + 17, 4, maxima, g)
            put(16 * g + ST_LAG + 18, 0, outputs_a, g)
            put(16 * g + ST_LAG + 19, 5, outputs_b, g)
        for n in range(NI):
            put(n, 2, scores, n)
            put(n + ST_LAG, 4, turned, n)
        for m in range(NI // 4):
            put(4 * m + ST_LAG + 5, 5, values, m)
        for s in range(START + 8, 0):
            put(s, 3, pump, 0, 3000)
        for s in range(0, NI + 70):
            for half in range(2):
                put(s, 3 + 2 * half, pump, half)
        while plan:
            now[0] = min(plan)
            for order, k, fn, args in sorted(plan.pop(now[0]), key=lambda t: t[:2]):
                fn(*args)
        SP.do(lambda e: e.nop(), [("store", NB - 1)])

        block = ctx.enter_context(nc.Block())

        @block.tensor
        def _(e):
            PE.emit(e)

        @block.vector
        def _(e):
            DV.emit(e)

        @block.scalar
        def _(e):
            AC.emit(e)

        @block.gpsimd
        def _(e):
            PO.emit(e)

        @block.sync
        def _(e):
            SP.emit(e)


def kernel(**inputs):
    import numpy as _np
    import concourse.bacc as _bacc
    from concourse import mybir as _mybir
    from concourse.bass_utils import run_bass_kernel_spmd as _run

    t = {k: _np.ascontiguousarray(v) for k, v in inputs.items()}

    def heads(w):
        s = w.shape[:-1]
        return w.reshape(*s, -1, 4, 16).swapaxes(-1, -2).reshape(*s, -1)

    wqkv, bqkv = t["L0_ffn_W_qkv"], t["L0_ffn_b_qkv"]
    lay = {
        "x": t["L0_attn_x"],
        "wqk": heads(wqkv[:, 0:512]),
        "bqk": heads(bqkv[0:512]).reshape(4, 128).T,
        "wvg": _np.concatenate([wqkv[:, 512:768], t["L0_ffn_W_gate"]], axis=1),
        "bv": bqkv[512:768].reshape(1, 256),
        "bg": _np.broadcast_to(t["L0_ffn_b_gate"], (128, 8)),
        "win": t["L0_attn_W_in"],
        "bin": _np.broadcast_to(t["L0_attn_b_in"], (4, 512)),
        "cw": t["L0_attn_conv_w"].reshape(4, 128, 4).transpose(1, 0, 2),
        "cwt": t["L0_attn_conv_w"].T,
        "cb": t["L0_attn_conv_b"].reshape(1, 512),
        "A": t["L0_attn_A"],
        "AT": t["L0_attn_A"].T,
        "Bp": t["L0_attn_Bp"],
        "Cp": t["L0_attn_Cp"],
        "Dp": t["L0_attn_Dp"],
        "wout": t["L0_attn_W_out"],
        "bout": t["L0_attn_b_out"].reshape(1, 256),
        "wexp": t["L0_ffn_W_experts"].transpose(1, 0, 2).reshape(256, 2048),
        "bexp": t["L0_ffn_b_experts"],
    }
    nc = _bacc.Bacc("TRN2", target_bir_lowering=False, num_devices=1)
    arrays, args = {}, []
    for name, a in lay.items():
        a = _np.ascontiguousarray(a)
        arrays[f"in_{name}"] = a
        args.append(nc.dram_tensor(f"in_{name}", a.shape, _mybir.dt.from_np(a.dtype), kind="ExternalInput").ap())
    o = nc.dram_tensor("out_0", (8, 512, 256), _mybir.dt.float32, kind="ExternalOutput").ap()
    kd = nc.dram_tensor("kd", (1, 768), _mybir.dt.float32, kind="Internal").ap()
    rd = nc.dram_tensor("rd", (128, 896), _mybir.dt.float32, kind="Internal").ap()
    program(nc, *args, o, kd, rd)
    r = _run(nc, [arrays], core_ids=[0])
    return r.results[0]["out_0"]
```
